# Optimizing a Trainium2 kernel written in Bass

```python
import numpy as np
import jax
import jax.numpy as jnp

def _softmax(x, axis=-1):
    return jax.nn.softmax(x, axis=axis)

def _gelu(x):
    return jax.nn.gelu(x, approximate=True)

def _silu(x):
    return jax.nn.silu(x)

def _sigmoid(x):
    return jax.nn.sigmoid(x)

def _layernorm(x, axis=-1, eps=1e-05):
    m = jnp.mean(x, axis=axis, keepdims=True)
    v = jnp.var(x, axis=axis, keepdims=True)
    return (x - m) / jnp.sqrt(v + eps)

def _scatter_add(tgt, idx, src, axis=0):
    return tgt.at[idx].add(src)

def _segment_sum(src, seg, n):
    return jax.ops.segment_sum(src, seg, n)
kernel_name = 'mk_adj_ffn_d2_adj_r2_c5506e'

def setup_inputs(seed: int=0):
    np.random.seed(seed)
    _w = jnp.asarray

    def _rec_inputs():
        import jax
        import jax.numpy as jnp
        _gk = jax.random.key(seed)
        x = -0.0002928 + 1 * jax.random.normal(jax.random.fold_in(_gk, 1), (16, 512, 128), jnp.float32)
        _a = jax.random.bernoulli(jax.random.fold_in(_gk, 2), 0.03125, (16, 512, 512))
        _a = jnp.logical_or(_a, jnp.swapaxes(_a, -1, -2))
        _a = jnp.logical_or(_a, jnp.eye(512, dtype=bool))
        adj = _a.astype(jnp.int32)
        return (x, adj)
    x, adj = _rec_inputs()

    def _L0_gnn_setup():
        import jax, jax.numpy as jnp
        import numpy as np
        B, N, F_IN, F_OUT = (8, 1024, 128, 128)
        ALPHA = 0.2
        NEG_BIG = -9000000000000000.0
        key = jax.random.key(seed)
        k1, k2, k3, k4 = jax.random.split(key, 4)
        x = jax.random.normal(k1, (B, N, F_IN), dtype=jnp.float32)
        adj = jax.random.randint(k2, (B, N, N), 0, 2, dtype=jnp.int32)
        gain = 1.414
        lim_W = gain * np.sqrt(6.0 / (F_IN + F_OUT))
        W = jax.random.uniform(k3, (F_IN, F_OUT), dtype=jnp.float32, minval=-lim_W, maxval=lim_W)
        lim_a = gain * np.sqrt(6.0 / (2 * F_OUT + 1))
        a = jax.random.uniform(k4, (2 * F_OUT, 1), dtype=jnp.float32, minval=-lim_a, maxval=lim_a)
        return {'x': x, 'adj': adj, 'W': W, 'a': a}
    _L0_gnn_all = _L0_gnn_setup()
    _L0_gnn_in = {k: v for k, v in _L0_gnn_all.items() if k in ('W', 'a')}
    del _L0_gnn_all

    def _L0_ffn_setup():
        import jax, jax.numpy as jnp
        import numpy as np
        B, S, D, E, H, K = (4, 2048, 128, 8, 256, 2)
        key = jax.random.key(seed)
        ks = jax.random.split(key, 6)
        x = jax.random.normal(ks[0], (B, S, D), jnp.float32)
        Wg = jax.random.normal(ks[1], (D, E), jnp.float32) * 0.02
        bg = jnp.zeros((E,), jnp.float32)
        W1 = jax.random.normal(ks[2], (E, D, H), jnp.float32) * 0.02
        b1 = jnp.zeros((E, H), jnp.float32)
        W2 = jax.random.normal(ks[3], (E, H, D), jnp.float32) * 0.02
        b2 = jnp.zeros((E, D), jnp.float32)
        return {'x': x, 'Wg': Wg, 'bg': bg, 'W1': W1, 'b1': b1, 'W2': W2, 'b2': b2}
    _L0_ffn_all = _L0_ffn_setup()
    _L0_ffn_in = {k: v for k, v in _L0_ffn_all.items() if k in ('Wg', 'bg', 'W1', 'b1', 'W2', 'b2')}
    del _L0_ffn_all

    def _L1_gnn_setup():
        import jax, jax.numpy as jnp
        import numpy as np
        ALPHA = 0.2
        key = jax.random.key(seed)
        k1, k2, k3, k4 = jax.random.split(key, 4)
        B, N, F_IN, F_OUT = (4, 2048, 128, 128)
        h = jax.random.normal(k1, (B, N, F_IN), dtype=jnp.float32)
        adj = jax.random.randint(k2, (B, N, N), 0, 2, dtype=jnp.int32)
        std_W = 1.414 * np.sqrt(2.0 / (F_IN + F_OUT))
        W = jax.random.normal(k3, (F_IN, F_OUT), dtype=jnp.float32) * std_W
        std_a = 1.414 * np.sqrt(2.0 / (1 + 2 * F_OUT))
        a = jax.random.normal(k4, (1, 2 * F_OUT), dtype=jnp.float32) * std_a
        return {'h': h, 'adj': adj, 'W': W, 'a': a}
    _L1_gnn_all = _L1_gnn_setup()
    _L1_gnn_in = {k: v for k, v in _L1_gnn_all.items() if k in ('W', 'a')}
    del _L1_gnn_all

    def _L1_ffn_setup():
        import jax, jax.numpy as jnp
        import numpy as np
        DIM = 128
        HEADS = 8
        NUM_KEYS = 128
        NUM_KV = NUM_KEYS ** 2
        PK_TOPK = 16
        FINAL_TOPK = 16
        DIM_KEY = DIM // 2
        P = 2

        def _pk(x, Wq_pk, pk_keys):
            b, n, _ = x.shape
            q = (x @ Wq_pk).reshape(b, n, P, HEADS, DIM_KEY).transpose(2, 0, 1, 3, 4)
            sim = jnp.einsum('pbnhd,pkhd->pbnhk', q, pk_keys)
            scores, idx = jax.lax.top_k(sim, PK_TOPK)
            idx0 = idx[0]
            idx1 = idx[1] * NUM_KEYS
            index = (idx0[..., :, None] + idx1[..., None, :]).reshape(b, n, HEADS, PK_TOPK * PK_TOPK)
            score = (scores[0][..., :, None] + scores[1][..., None, :]).reshape(b, n, HEADS, PK_TOPK * PK_TOPK)
            final_scores, pk_idx = jax.lax.top_k(score, FINAL_TOPK)
            final_indices = jnp.take_along_axis(index, pk_idx, axis=-1)
            final_scores = jax.nn.softmax(final_scores, axis=-1)
            return (final_scores, final_indices)
        key = jax.random.key(seed)
        ks = jax.random.split(key, 7)
        b, n = (2, 512)
        std = 0.02
        x = jax.random.normal(ks[0], (b, n, DIM), dtype=jnp.float32)
        Wq_pk = jax.random.normal(ks[1], (DIM, P * HEADS * DIM_KEY), dtype=jnp.float32) * std
        pk_keys = jax.random.normal(ks[2], (P, NUM_KEYS, HEADS, DIM_KEY), dtype=jnp.float32) * std
        Wq = jax.random.normal(ks[3], (DIM, HEADS * DIM), dtype=jnp.float32) * std
        keys_table = jax.random.normal(ks[4], (NUM_KV * HEADS, DIM), dtype=jnp.float32) * std
        values_table = jax.random.normal(ks[5], (NUM_KV * HEADS, DIM), dtype=jnp.float32) * std
        Wo = jax.random.normal(ks[6], (DIM * HEADS, DIM), dtype=jnp.float32) * std
        return {'x': x, 'Wq_pk': Wq_pk, 'pk_keys': pk_keys, 'Wq': Wq, 'keys_table': keys_table, 'values_table': values_table, 'Wo': Wo}
    _L1_ffn_all = _L1_ffn_setup()
    _L1_ffn_in = {k: v for k, v in _L1_ffn_all.items() if k in ('Wq_pk', 'pk_keys', 'Wq', 'keys_table', 'values_table', 'Wo')}
    del _L1_ffn_all
    return {'x': x, 'adj': adj, 'L0_gnn_W': _L0_gnn_in['W'], 'L0_gnn_a': _L0_gnn_in['a'], 'L0_ffn_Wg': _L0_ffn_in['Wg'], 'L0_ffn_bg': _L0_ffn_in['bg'], 'L0_ffn_W1': _L0_ffn_in['W1'], 'L0_ffn_b1': _L0_ffn_in['b1'], 'L0_ffn_W2': _L0_ffn_in['W2'], 'L0_ffn_b2': _L0_ffn_in['b2'], 'L1_gnn_W': _L1_gnn_in['W'], 'L1_gnn_a': _L1_gnn_in['a'], 'L1_ffn_Wq_pk': _L1_ffn_in['Wq_pk'], 'L1_ffn_pk_keys': _L1_ffn_in['pk_keys'], 'L1_ffn_Wq': _L1_ffn_in['Wq'], 'L1_ffn_keys_table': _L1_ffn_in['keys_table'], 'L1_ffn_values_table': _L1_ffn_in['values_table'], 'L1_ffn_Wo': _L1_ffn_in['Wo']}

def reference(x, adj, L0_gnn_W, L0_gnn_a, L0_ffn_Wg, L0_ffn_bg, L0_ffn_W1, L0_ffn_b1, L0_ffn_W2, L0_ffn_b2, L1_gnn_W, L1_gnn_a, L1_ffn_Wq_pk, L1_ffn_pk_keys, L1_ffn_Wq, L1_ffn_keys_table, L1_ffn_values_table, L1_ffn_Wo):
    import jax
    import jax.numpy as jnp

    def _L0_gnn_ref(x, adj, W, a):
        import jax, jax.numpy as jnp
        import numpy as np
        B, N, F_IN, F_OUT = (8, 1024, 128, 128)
        ALPHA = 0.2
        NEG_BIG = -9000000000000000.0
        h = jnp.einsum('bnf,fo->bno', x, W)
        a1 = a[:F_OUT, 0]
        a2 = a[F_OUT:, 0]
        s1 = h @ a1
        s2 = h @ a2
        e = jax.nn.leaky_relu(s1[:, :, None] + s2[:, None, :], negative_slope=ALPHA)
        att = jnp.where(adj > 0, e, jnp.float32(NEG_BIG))
        att = jax.nn.softmax(att, axis=1)
        h_prime = jnp.einsum('bij,bjo->bio', att, h)
        return jax.nn.elu(h_prime)

    def _L0_ffn_ref(x, Wg, bg, W1, b1, W2, b2):
        import jax, jax.numpy as jnp
        import numpy as np
        B, S, D, E, H, K = (4, 2048, 128, 8, 256, 2)
        Bv, Sv, Dv = x.shape
        gate_scores = x @ Wg + bg
        _, idx = jax.lax.top_k(gate_scores, K)
        mask = jax.nn.one_hot(idx, E, dtype=x.dtype).sum(axis=-2)
        xf = x.reshape(-1, Dv)
        mf = mask.reshape(-1, E)
        h = jax.nn.gelu(jnp.einsum('td,edh->teh', xf, W1) + b1[None], approximate=False)
        y = jnp.einsum('teh,ehd->ted', h, W2) + b2[None]
        out = jnp.einsum('ted,te->td', y, mf)
        return out.reshape(Bv, Sv, Dv)

    def _L1_gnn_ref(h, adj, W, a):
        import jax, jax.numpy as jnp
        import numpy as np
        ALPHA = 0.2
        F_out = W.shape[1]
        Hh = jnp.einsum('bni,io->bno', h, W)
        a_src = a[0, :F_out]
        a_dst = a[0, F_out:]
        s = jnp.einsum('bno,o->bn', Hh, a_src)
        d = jnp.einsum('bno,o->bn', Hh, a_dst)
        logits = s[:, :, None] + d[:, None, :]
        e = jnp.where(adj != 0, jnp.exp(-jax.nn.leaky_relu(logits, negative_slope=ALPHA)), jnp.zeros((), dtype=Hh.dtype))
        rowsum = jnp.sum(e, axis=-1, keepdims=True)
        rowsum = jnp.where(rowsum == 0.0, 1.0, rowsum)
        h_prime = jnp.einsum('bnm,bmo->bno', e, Hh) / rowsum
        return jax.nn.elu(h_prime)

    def _L1_ffn_ref(x, Wq_pk, pk_keys, Wq, keys_table, values_table, Wo):
        import jax, jax.numpy as jnp
        import numpy as np
        DIM = 128
        HEADS = 8
        NUM_KEYS = 128
        NUM_KV = NUM_KEYS ** 2
        PK_TOPK = 16
        FINAL_TOPK = 16
        DIM_KEY = DIM // 2
        P = 2

        def _pk(x, Wq_pk, pk_keys):
            b, n, _ = x.shape
            q = (x @ Wq_pk).reshape(b, n, P, HEADS, DIM_KEY).transpose(2, 0, 1, 3, 4)
            sim = jnp.einsum('pbnhd,pkhd->pbnhk', q, pk_keys)
            scores, idx = jax.lax.top_k(sim, PK_TOPK)
            idx0 = idx[0]
            idx1 = idx[1] * NUM_KEYS
            index = (idx0[..., :, None] + idx1[..., None, :]).reshape(b, n, HEADS, PK_TOPK * PK_TOPK)
            score = (scores[0][..., :, None] + scores[1][..., None, :]).reshape(b, n, HEADS, PK_TOPK * PK_TOPK)
            final_scores, pk_idx = jax.lax.top_k(score, FINAL_TOPK)
            final_indices = jnp.take_along_axis(index, pk_idx, axis=-1)
            final_scores = jax.nn.softmax(final_scores, axis=-1)
            return (final_scores, final_indices)
        b, n, d = x.shape
        q = (x @ Wq).reshape(b, n, HEADS, DIM) * DIM ** (-0.5)
        kv_scores, indices = _pk(x, Wq_pk, pk_keys)
        offsets = jnp.arange(HEADS, dtype=indices.dtype) * NUM_KV
        ind = indices + offsets[None, None, :, None]
        k = jnp.einsum('bnhk,bnhkd->bnhd', kv_scores, keys_table[ind])
        v = jnp.einsum('bnhk,bnhkd->bnhd', kv_scores, values_table[ind])
        sim = jnp.einsum('bihd,bjhd->bhij', q, k)
        neg = -jnp.finfo(sim.dtype).max
        causal = jnp.tril(jnp.ones((n, n), dtype=bool))
        sim = jnp.where(causal, sim, neg)
        attn = jax.nn.softmax(sim, axis=-1)
        out = jnp.einsum('bhij,bjhd->bhid', attn, v)
        out = out.transpose(0, 2, 1, 3).reshape(b, n, HEADS * DIM)
        return out @ Wo
    x = x + _L0_gnn_ref(_layernorm(x, axis=-1), adj, L0_gnn_W, L0_gnn_a)
    x = x + _L0_ffn_ref(_layernorm(x, axis=-1), L0_ffn_Wg, L0_ffn_bg, L0_ffn_W1, L0_ffn_b1, L0_ffn_W2, L0_ffn_b2)
    x = x + _L1_gnn_ref(_layernorm(x, axis=-1), adj, L1_gnn_W, L1_gnn_a)
    x = x + _L1_ffn_ref(_layernorm(x, axis=-1), L1_ffn_Wq_pk, L1_ffn_pk_keys, L1_ffn_Wq, L1_ffn_keys_table, L1_ffn_values_table, L1_ffn_Wo)
    return x

_drawn_inputs = setup_inputs


def setup_inputs(seed=0):
    import zlib

    import numpy as np

    out = dict(_drawn_inputs(seed))
    spreads = {'L0_ffn_bg': (0.0, 0.1), 'L0_ffn_b1': (0.0, 0.342), 'L0_ffn_b2': (0.0, 0.1)}
    factors = {'L1_ffn_Wq_pk': 8.0,
     'L1_ffn_pk_keys': 8.0,
     'L1_ffn_Wq': 64.0,
     'L1_ffn_keys_table': 64.0,
     'L1_ffn_values_table': 8.0,
     'L1_ffn_Wo': 8.0}
    for name, (base, spread) in spreads.items():
        noise = np.random.default_rng([zlib.crc32(name.encode()), seed]).standard_normal(out[name].shape)
        drawn = base * np.exp(spread * noise) if base else spread * noise
        out[name] = jnp.asarray(drawn.astype(out[name].dtype))
    for name, factor in factors.items():
        out[name] = (out[name] * factor).astype(out[name].dtype)
    return out
```

```python
from contextlib import ExitStack

import numpy as np

import concourse.bass as bass
from concourse import mybir

F32 = mybir.dt.float32
I32 = mybir.dt.int32
U32 = mybir.dt.uint32
ALU = mybir.AluOpType
ACT = mybir.ActivationFunctionType
AX = mybir.AxisListType
ds = bass.ds

P = 128
B, N, D = 16, 512, 128
NT = N // P
E, HID = 8, 256
HC = HID // P
NH, DK, NKEY = 8, 64, 128
TOPK = 16
NKV = NKEY * NKEY
RECTS = [(0, 1, 16), (1, 1, 8), (2, 2, 5), (4, 4, 3), (8, 8, 1)]
NC = sum(na * nb for _, na, nb in RECTS)
EPS = 1e-5
SLOPE = 0.2
NEG_BIG = -9000000000000000.0
CAUSAL_NEG = -1e30
LOWEST = -3.0e38
RING = 2 * TOPK
HEADS = B * NH
HX = D + 2


def program(nc, x, adjT, wgT0, wgT1, wg0, wg1, ac0, ac1, gate_w, gate_b, w1, b1, w2, b2,
            wpkT, keysT, wq, table, wo, out):
    ctx = ExitStack()
    with ctx:
        def sb(name, shape, dt=F32):
            return ctx.enter_context(nc.sbuf_tensor(name, shape, dt))

        def sem(name):
            return ctx.enter_context(nc.semaphore(name))

        ident = sb("ident", [P, P])
        causal = sb("causal", [P, P])
        iota_i = sb("iota_i", [P, NC], I32)
        iota = sb("iota", [P, NC])
        head_row_i = sb("head_row_i", [P, NH], I32)
        head_row = sb("head_row", [P, NH])
        ones = sb("ones", [1, P])
        b2_sb = sb("b2_sb", [1, E * D])
        gb_sb = sb("gb_sb", [1, E])
        gw_sb = sb("gw_sb", [P, E])
        b1_sb = sb("b1_sb", [P, E, HC])
        w1_sb = sb("w1_sb", [P, E, HID])
        w2_sb = sb("w2_sb", [P, E, HC, D])
        ac_sb = sb("ac_sb", [P, 2, 2])
        wx = sb("wx", [P, 2, HX])
        wsrc = sb("wsrc", [P, 2, P])
        pk_w = sb("pk_w", [P, NH * 2 * NKEY])
        wq_sb = sb("wq_sb", [P, NH * D])
        wo_sb = sb("wo_sb", [P, NH * D])

        xb = sb("xb", [P, 2, NT, D])
        adj_sb = sb("adj_sb", [P, 2, NT, N], I32)
        neg = sb("neg", [P, NT, N])
        att = sb("att", [P, NT, N])
        xn = sb("xn", [P, NT, D])
        xT = sb("xT", [P, N])
        hx = sb("hx", [P, NT, HX])
        hid = sb("hid", [P, 4, N])
        ex = hid[:, 0, :].rearrange("p (a b) -> p a b", b=D)
        stats = sb("stats", [P, NT, 6])
        mv = sb("mv", [P, NT, 2])
        var_e = sb("var_e", [P, NT])
        std = sb("std", [P, NT])
        rstd = sb("rstd", [P, NT])
        colmax = sb("colmax", [P, NT])
        ncolmax = sb("ncolmax", [P, NT])
        colsum = sb("colsum", [P, NT])
        rcol = sb("rcol", [P, NT])
        rowsum = sb("rowsum", [P, NT])
        logits = sb("logits", [P, NT, E])
        top8 = sb("top8", [P, NT, 8])
        top8_i = sb("top8_i", [P, NT, 8], U32)
        top8_f = sb("top8_f", [P, NT, 8])
        gate = sb("gate", [P, NT, E])

        xnT = sb("xnT", [P, B * N])
        xs = sb("xs", [P, 2, N])
        wqs = sb("wqs", [P, 2, D])
        qT = sb("qT", [P, 2, N])
        kT = sb("kT", [P, 2, N])
        vv = sb("vv", [P, 2, NT, D])
        rows = sb("rows", [P, RING, 2 * D])
        diag = sb("diag", [P, TOPK, P])
        prob = sb("prob", [P, 2, N])
        probT = sb("probT", [P, NT, N])
        oT = sb("oT", [P, N])
        yb = sb("yb", [P, 2 * NT, D])
        half = sb("half", [P, 2, 2, TOPK])
        half_i = sb("half_i", [P, 2, TOPK], U32)
        rest = sb("rest", [P, 2, NKEY])
        cand = sb("cand", [P, 2, NC])
        cand2 = sb("cand2", [P, NC])
        best = sb("best", [P, 2, NT, TOPK])
        nbest = sb("nbest", [P, 2, NT])
        pos_i = sb("pos_i", [P, TOPK], U32)
        pos = sb("pos", [P, TOPK])
        pick = sb("pick", [P, TOPK, NC])
        row_f = sb("row_f", [P, TOPK])
        row_i = sb("row_i", [P, 2, NT, TOPK], U32)
        wexp = sb("wexp", [P, 2, NT, TOPK])
        wsum = sb("wsum", [P, 2, NT])
        wrec = sb("wrec", [P, NT])
        wgt = sb("wgt", [P, 2, NT, TOPK])
        nrow = sb("nrow", [P, NT])
        psum_row = sb("psum_row", [P, NT])
        prec = sb("prec", [P, NT])

        wpkT_sb = rows[0:DK, 0:8, :].rearrange("p a b -> p (a b)")
        keysT_sb = rows[0:DK, 8:16, :].rearrange("p a b -> p (a b)")
        wgT_sb = [rows[:, 16 + g, 0:D] for g in range(2)]

        bank = [ctx.enter_context(nc.psum_tensor(f"bank{i}", [P, 512], F32)) for i in range(8)]
        tr_ps = bank[0]
        hx_ps = [bank[1], bank[2]]
        src_ps = bank[3]
        msg_ps = [bank[4], bank[5]]
        up_ps = [bank[5], bank[6]]
        down_ps = [bank[1], bank[2]]
        gate_ps = bank[3]
        sim_ps = [bank[0], bank[1]]
        k_ps, v_ps = bank[2], bank[3]
        s_ps = [bank[4], bank[5]]
        pT_ps = bank[6]
        qoy_ps = bank[7]

        turn_pool, turn_dve, turn_sp = sem("turn_pool"), sem("turn_dve"), sem("turn_sp")
        weights_in = sem("weights_in")
        made = sem("made")
        consts = sem("consts")
        setup_mm, setup_cp = sem("setup_mm"), sem("setup_cp")
        chain = sem("chain")
        x_in = [sem(f"x_in{i}") for i in range(2)]
        adj_in = [sem(f"adj_in{i}") for i in range(2)]
        x_out = [sem(f"x_out{i}") for i in range(2)]
        var_ready, std_ready, xn_ready = sem("var_ready"), sem("std_ready"), sem("xn_ready")
        tr_ready, xT_ready = sem("tr_ready"), sem("xT_ready")
        src_ready, hx_ready, hx_copied = sem("src_ready"), sem("hx_ready"), sem("hx_copied")
        z_ready, masked, att_ready = sem("z_ready"), sem("masked"), sem("att_ready")
        rhs_ready, msg_ready = sem("rhs_ready"), sem("msg_ready")
        elu_in, elu_exp = sem("elu_in"), sem("elu_exp")
        gate_ready, up_ready, gelu_done = sem("gate_ready"), sem("up_ready"), sem("gelu_done")
        down_ready, down_used = sem("down_ready"), sem("down_used")
        x3_ready, front_done = sem("x3_ready"), sem("front_done")
        y_in, y_out = sem("y_in"), sem("y_out")
        xs_ready, q_ready, q_copied = sem("xs_ready"), sem("q_ready"), sem("q_copied")
        sim_ready, sim_used = sem("sim_ready"), sem("sim_used")
        best_ready, wexp_ready, wgt_ready = sem("best_ready"), sem("wexp_ready"), sem("wgt_ready")
        row_ready = sem("row_ready")
        row_in = [sem(f"row_in{i}") for i in range(RING)]
        diag_ready, kv_step, kv_copied = sem("diag_ready"), sem("kv_step"), sem("kv_copied")
        s_ready, max_ready, p_ready = sem("s_ready"), sem("max_ready"), sem("p_ready")
        pT_ready, pT_copied = sem("pT_ready"), sem("pT_copied")
        o_ready, o_copied, y_ready, y_used = sem("o_ready"), sem("o_copied"), sem("y_ready"), sem("y_used")

        STEP0 = 2 * TOPK

        x_v = x.rearrange("(n p) d -> p n d", p=P)
        adj_v = adjT.rearrange("(n p) i -> p n i", p=P)
        out_v = out.rearrange("(n p) d -> p n d", p=P)
        x3_dram = nc.dram_tensor("x3_dram", [B * N, D], F32, kind="Internal").ap()
        x3_v = x3_dram.rearrange("(n p) d -> p n d", p=P)

        weight_loads = [
            (ac_sb[:, 0, :], ac0), (ac_sb[:, 1, :], ac1), (wgT_sb[0], wgT0), (wgT_sb[1], wgT1),
            (wx[:, 0, 0:D], wg0), (wx[:, 1, 0:D], wg1), (gw_sb[:, :], gate_w), (gb_sb[:, :], gate_b),
            (w1_sb[:, :, :], w1), (b1_sb[:, :, :], b1), (w2_sb[:, :, :, :], w2), (b2_sb[:, :], b2),
            (wpkT_sb, wpkT), (keysT_sb, keysT), (wq_sb[:, :], wq), (wo_sb[:, :], wo),
        ]
        WEIGHTS = 16 * len(weight_loads)

        block = ctx.enter_context(nc.Block())

        @block.sync
        def _(sp):
            for dst, src in weight_loads:
                sp.dma_start(dst, src).then_inc(weights_in, 16)

            def load_front(b, par):
                sp.dma_start(xb[:, par, :, :], x_v[:, ds(NT * b, NT), :]).then_inc(x_in[par], 16)
                sp.dma_start(adj_sb[:, par, :, :], adj_v[:, ds(NT * b, NT), :]).then_inc(adj_in[par], 16)

            def store_front(i, par):
                b = 2 * i + par
                sp.wait_ge(x3_ready, b + 1)
                sp.dma_start(x3_v[:, ds(NT * b, NT), :], xb[:, par, :, :]).then_inc(x_out[par], 16)
                sp.wait_ge(x_out[par], 16 * (i + 1))

            load_front(0, 0)
            load_front(1, 1)
            with sp.Fori(0, B // 2 - 1) as i:
                for par in range(2):
                    store_front(i, par)
                    sp.wait_ge(front_done, 2 * i + par + 1)
                    load_front(2 * i + par + 2, par)
            for par in range(2):
                store_front(B // 2 - 1, par)

            def load_y(b):
                sp.dma_start(yb[:, ds(NT * (b % 2), NT), :], x3_v[:, ds(NT * b, NT), :]).then_inc(y_in, 16)
                sp.wait_ge(y_in, 16 * (b + 1))
                sp.sem_inc(turn_sp, 1)

            def store_y(b):
                sp.wait_ge(y_used, NH * (b + 1) + 1)
                sp.dma_start(out_v[:, ds(NT * b, NT), :], yb[:, ds(NT * (b % 2), NT), :]).then_inc(y_out, 16)
                sp.wait_ge(y_out, 16 * (b + 1))
                sp.sem_inc(turn_sp, 1)

            load_y(0)
            load_y(1)
            with sp.Fori(0, B - 2) as b:
                store_y(b)
                load_y(b + 2)
            store_y(B - 2)
            store_y(B - 1)

        @block.gpsimd
        def _(pool):
            pool.memset(ident[:, :], 0.0).then_inc(made, 1)
            pool.memset(causal[:, :], 0.0).then_inc(made, 1)
            pool.wait_ge(made, 2)
            pool.affine_select(out=ident[:, :], in_=ident[:, :], compare_op=ALU.not_equal, fill=1.0,
                               base=0, pattern=[[-1, P]], channel_multiplier=1).then_inc(made, 1)
            pool.affine_select(out=causal[:, :], in_=causal[:, :], compare_op=ALU.is_ge, fill=CAUSAL_NEG,
                               base=0, pattern=[[-1, P]], channel_multiplier=1).then_inc(made, 1)
            pool.iota(iota_i[:, :], [[1, NC]], base=0, channel_multiplier=0).then_inc(made, 1)
            pool.iota(head_row_i[:, :], [[NKV // 2, NH]], base=0, channel_multiplier=0).then_inc(made, 1)
            pool.wait_ge(made, 6)

            def gathers(i, par):
                for t in range(NT):
                    n = NT * (2 * i + par) + t
                    pool.wait_ge(kv_step, TOPK * n + STEP0 - TOPK)
                    pool.wait_ge(row_ready, n + 1)
                    pool.sem_inc(turn_pool, 1)
                    for k in range(TOPK):
                        slot = TOPK * (t % 2) + k
                        pool.indirect_dma_start(
                            rows[:, slot, :], None, table,
                            bass.IndirectOffsetOnAxis(ap=row_i[:, par, t, k:k + 1], axis=0),
                        ).then_inc(row_in[slot], 16)

            with pool.Fori(0, HEADS // 2) as i:
                for par in range(2):
                    gathers(i, par)

        @block.tensor
        def _(pe):
            mm = nc.tensor.matmul
            pe.wait_ge(weights_in, WEIGHTS)
            for g in range(2):
                mm(bank[7][:, 2 * g:2 * g + 2], wgT_sb[g], ac_sb[:, g, :], start=True, stop=True)\
                    .then_inc(setup_mm, 1)
            for c in range(NH * 2):
                mm(bank[c // 4][:, (c % 4) * P:(c % 4 + 1) * P], wpkT_sb[:, c * P:(c + 1) * P],
                   keysT_sb[:, c * P:(c + 1) * P], start=True, stop=True).then_inc(setup_mm, 1)
            pe.sem_inc(kv_step, STEP0)
            pe.sem_inc(tr_ready, 1)
            pe.wait_ge(setup_cp, 1)
            pe.wait_ge(made, 6)

            def transposed(n):
                pe.wait_ge(xn_ready, n + 1)
                pe.wait_ge(xT_ready, n + 1)
                for t in range(NT):
                    last = nc.tensor.transpose(tr_ps[:, t * P:(t + 1) * P], xn[:, t, :], ident[:, :])
                last.then_inc(tr_ready, 1)

            def graph(b, g):
                pe.wait_ge(xT_ready, 4 * b + 2 * g + 2)
                mm(src_ps[:, :], wsrc[:, g, :], xT[:, :], start=True, stop=True).then_inc(src_ready, 1)
                for t in range(NT):
                    last = mm(hx_ps[t // 2][:, (t % 2) * HX:(t % 2 + 1) * HX], xT[:, t * P:(t + 1) * P],
                              wx[:, g, :], start=True, stop=True)
                last.then_inc(hx_ready, 1)
                width = D + g
                pe.wait_ge(rhs_ready, 2 * b + g + 1)
                pe.wait_ge(att_ready, NT * (2 * b + g + 1))
                for it in range(NT):
                    for jt in range(NT):
                        last = mm(msg_ps[it // 2][:, (it % 2) * HX:(it % 2) * HX + width],
                                  att[:, jt, it * P:(it + 1) * P], hx[:, jt, 0:width],
                                  start=(jt == 0), stop=(jt == NT - 1))
                last.then_inc(msg_ready, 1)

            def experts(b):
                pe.wait_ge(xT_ready, 4 * b + 3)
                for t in range(NT):
                    o = gate_ps[:, t * E:(t + 1) * E]
                    mm(o, xT[:, t * P:(t + 1) * P], gw_sb[:, :], start=True, stop=False)
                    last = mm(o, ones[:, :], gb_sb[:, :], start=False, stop=True)
                last.then_inc(gate_ready, 1)

                def down(e):
                    pe.wait_ge(gelu_done, HC * (E * b + e + 1))
                    if e >= 2:
                        pe.wait_ge(down_used, E * b + e - 1)
                    for t in range(NT):
                        o = down_ps[e % 2][:, t * P:(t + 1) * P]
                        for c in range(HC):
                            mm(o, hid[:, (HC * e + c) % 4, t * P:(t + 1) * P], w2_sb[:, e, c, :],
                               start=(c == 0), stop=False)
                        last = mm(o, ones[:, :], b2_sb[:, e * D:(e + 1) * D], start=False, stop=True)
                    last.then_inc(down_ready, 1)

                for e in range(E):
                    for c in range(HC):
                        u = HC * e + c
                        if u >= 2:
                            pe.wait_ge(gelu_done, HC * E * b + u - 1)
                        mm(up_ps[u % 2][:, :], w1_sb[:, e, c * P:(c + 1) * P], xT[:, :],
                           start=True, stop=True).then_inc(up_ready, 1)
                    if e >= 1:
                        down(e - 1)
                down(E - 1)

            with pe.Fori(0, B) as b:
                transposed(4 * b)
                graph(b, 0)
                transposed(4 * b + 1)
                experts(b)
                transposed(4 * b + 2)
                graph(b, 1)
                transposed(4 * b + 3)

            pe.wait_ge(xT_ready, 4 * B + 1)
            pe.wait_ge(front_done, B)

            def query(H, par):
                pe.wait_ge(xs_ready, H + 1)
                if not (isinstance(H, int) and H == 0):
                    pe.wait_ge(y_used, H)
                mm(qoy_ps[:, :], wqs[:, par, :], xs[:, par, :], start=True, stop=True).then_inc(q_ready, 1)

            def scores(H, par, t):
                first = isinstance(H, int) and H == 0
                if not first:
                    pe.wait_ge(sim_used, NT * H + t - 1)
                elif t >= 2:
                    pe.wait_ge(sim_used, t - 1)
                mm(sim_ps[t % 2][:, 0:2 * NKEY], xs[:, par, t * P:(t + 1) * P],
                   pk_w[:, ds((H % NH) * 2 * NKEY, 2 * NKEY)], start=True, stop=True).then_inc(sim_ready, 1)

            def combine(i, par, t):
                n = NT * (2 * i + par) + t
                pe.wait_ge(kv_copied, n + 1)
                for k in range(TOPK):
                    slot = TOPK * (t % 2) + k
                    if k % 8 == 0:
                        pe.wait_ge(diag_ready, 2 * n + 1 + k // 8)
                    use = 2 * par + t // 2
                    pe.wait_ge(row_in[slot], 16 * (4 * i + use + 1))
                    mm(k_ps[:, 0:P], rows[:, slot, 0:D], diag[:, k, :], start=(k == 0), stop=(k == TOPK - 1))
                    mm(v_ps[:, 0:D], diag[:, k, :], rows[:, slot, D:2 * D], start=(k == 0),
                       stop=(k == TOPK - 1)).then_inc(kv_step, 1)

            def attend(H, par, last_head):
                pe.wait_ge(kv_copied, NT * (H + 1) + 1)

                def s_tile(it):
                    if it >= 2:
                        pe.wait_ge(p_ready, NT * H + it - 1)
                    q = qT[:, par, it * P:(it + 1) * P]
                    if it:
                        mm(s_ps[it % 2][:, 0:it * P], q, kT[:, par, 0:it * P], start=True, stop=True)
                    o = s_ps[it % 2][:, it * P:(it + 1) * P]
                    mm(o, q, kT[:, par, it * P:(it + 1) * P], start=True, stop=False)
                    mm(o, ident[:, :], causal[:, :], start=False, stop=True).then_inc(s_ready, 1)

                def t_tile(it):
                    pe.wait_ge(p_ready, NT * H + it + 1)
                    if it:
                        pe.wait_ge(pT_copied, NT * H + it)
                    for jt in range(it + 1):
                        last = nc.tensor.transpose(pT_ps[:, jt * P:(jt + 1) * P],
                                                   prob[:, it % 2, jt * P:(jt + 1) * P], ident[:, :])
                    last.then_inc(pT_ready, 1)

                s_tile(0)
                s_tile(1)
                for it in range(NT):
                    t_tile(it)
                    if it + 2 < NT:
                        s_tile(it + 2)
                if not last_head:
                    pe.wait_ge(q_copied, H + 2)
                pe.wait_ge(pT_copied, NT * (H + 1))
                for it in range(NT):
                    for jt in range(it + 1):
                        last = mm(qoy_ps[:, it * P:(it + 1) * P], vv[:, par, jt, :],
                                  probT[:, jt, it * P:(it + 1) * P], start=(jt == 0), stop=(jt == it))
                last.then_inc(o_ready, 1)
                pe.wait_ge(o_copied, H + 1)
                for it in range(NT):
                    last = mm(qoy_ps[:, it * P:(it + 1) * P], oT[:, it * P:(it + 1) * P],
                              wo_sb[:, ds((H % NH) * D, D)], start=True, stop=True)
                last.then_inc(y_ready, 1)

            query(0, 0)
            for t in range(NT):
                scores(0, 0, t)

            def two_heads(i, last):
                for par in range(2):
                    H = 2 * i + par
                    more = not (last and par)
                    if more:
                        query(H + 1, 1 - par)
                    for t in range(NT):
                        if more:
                            scores(H + 1, 1 - par, t)
                        combine(i, par, t)
                    attend(H, par, not more)

            with pe.Fori(0, HEADS // 2 - 1) as i:
                two_heads(i, False)
            two_heads(HEADS // 2 - 1, True)

        @block.scalar
        def _(act):
            A = nc.scalar.activation
            act.sem_inc(kv_copied, 1)
            act.sem_inc(xT_ready, 1)
            act.wait_ge(weights_in, WEIGHTS)

            def std_dev(n):
                act.wait_ge(var_ready, n + 1)
                A(std[:, :], var_e[:, :], ACT.Sqrt).then_inc(std_ready, 1)

            def copy_xT(n, b=None):
                act.wait_ge(tr_ready, n + 2)
                dst = xT[:, :] if b is None else xnT[:, ds(N * b, N)]
                A(dst, tr_ps[:, :], ACT.Copy).then_inc(xT_ready, 1)

            def graph(b, g):
                act.wait_ge(hx_ready, 2 * b + g + 1)
                for q in range(2):
                    last = A(hx[:, 2 * q:2 * q + 2, :].rearrange("p a b -> p (a b)"),
                             hx_ps[q][:, 0:2 * HX], ACT.Copy)
                last.then_inc(hx_copied, 1)
                act.wait_ge(hx_copied, 2 * b + g + 1)
                for t in range(NT):
                    A(att[:, t, :], src_ps[:, :], ACT.Identity, bias=hx[:, t, D + 1:D + 2])\
                        .then_inc(z_ready, 1)
                for t in range(NT):
                    act.wait_ge(masked, NT * (2 * b + g) + t + 1)
                    if g == 0:
                        A(att[:, t, :], att[:, t, :], ACT.Exp, bias=ncolmax[:, t:t + 1],
                          accum_out=colsum[:, t:t + 1]).then_inc(att_ready, 1)
                    else:
                        A(att[:, t, :], att[:, t, :], ACT.Exp, scale=-1.0).then_inc(att_ready, 1)
                act.wait_ge(elu_in, 2 * b + g + 1)
                A(ex[:, :, :], ex[:, :, :], ACT.Exp).then_inc(elu_exp, 1)

            def experts(b):
                for u in range(HC * E):
                    act.wait_ge(up_ready, HC * E * b + u + 1)
                    if u >= 4:
                        act.wait_ge(down_ready, E * b + u // HC - 1)
                    A(hid[:, u % 4, :], up_ps[u % 2][:, :], ACT.Gelu,
                      bias=b1_sb[:, u // HC, u % HC:u % HC + 1]).then_inc(gelu_done, 1)

            with act.Fori(0, B) as b:
                std_dev(4 * b)
                copy_xT(4 * b)
                graph(b, 0)
                std_dev(4 * b + 1)
                copy_xT(4 * b + 1)
                experts(b)
                std_dev(4 * b + 2)
                copy_xT(4 * b + 2)
                graph(b, 1)
                std_dev(4 * b + 3)
                copy_xT(4 * b + 3, b)

            def query_in(H, par):
                A(xs[:, par, :], xnT[:, ds((H // NH) * N, N)], ACT.Copy)
                A(wqs[:, par, :], wq_sb[:, ds((H % NH) * D, D)], ACT.Copy).then_inc(xs_ready, 1)
                act.wait_ge(q_ready, H + 1)
                A(qT[:, par, :], qoy_ps[:, :], ACT.Copy, scale=float(D) ** -0.5).then_inc(q_copied, 1)

            def best_exp(H, par, t):
                act.wait_ge(best_ready, NT * H + t + 1)
                A(wexp[:, par, t, :], best[:, par, t, :], ACT.Exp, bias=nbest[:, par, t:t + 1],
                  accum_out=wsum[:, par, t:t + 1]).then_inc(wexp_ready, 1)

            def combine(i, par, t):
                n = NT * (2 * i + par) + t
                if t == 0:
                    act.wait_ge(wgt_ready, 2 * i + par + 1)
                for k in range(TOPK):
                    if k % 8 == 0:
                        act.wait_ge(kv_step, TOPK * n + k + 8 - TOPK + STEP0)
                    last = A(diag[:, k, :], ident[:, :], ACT.Copy, scale=wgt[:, par, t, k:k + 1])
                    if k % 8 == 7:
                        last.then_inc(diag_ready, 1)
                act.wait_ge(kv_step, TOPK * (n + 1) + STEP0)
                A(kT[:, par, t * P:(t + 1) * P], k_ps[:, 0:P], ACT.Copy)
                A(vv[:, par, t, :], v_ps[:, 0:D], ACT.Copy).then_inc(kv_copied, 1)

            def attend(H, par):
                for it in range(NT):
                    act.wait_ge(max_ready, NT * H + it + 1)
                    if it >= 2:
                        act.wait_ge(pT_ready, NT * H + it - 1)
                    w = (it + 1) * P
                    A(prob[:, it % 2, 0:w], s_ps[it % 2][:, 0:w], ACT.Exp, bias=nrow[:, it:it + 1],
                      accum_out=psum_row[:, it:it + 1]).then_inc(p_ready, 1)
                act.wait_ge(o_ready, H + 1)
                A(oT[:, :], qoy_ps[:, :], ACT.Copy).then_inc(o_copied, 1)

            query_in(0, 0)
            for t in range(NT):
                best_exp(0, 0, t)

            def two_heads(i, last):
                for par in range(2):
                    H = 2 * i + par
                    more = not (last and par)
                    if more:
                        query_in(H + 1, 1 - par)
                    for t in range(NT):
                        combine(i, par, t)
                        if more:
                            best_exp(H + 1, 1 - par, t)
                    attend(H, par)

            with act.Fori(0, HEADS // 2 - 1) as i:
                two_heads(i, False)
            two_heads(HEADS // 2 - 1, True)

        @block.vector
        def _(dve):
            V = nc.vector
            count = [0]

            def mark(ins):
                count[0] += 1
                ins.then_inc(chain, 1)
                return count[0]

            def after(value):
                dve.wait_ge(chain, value)

            def rewind():
                after(count[0])
                dve.sem_clear(chain)
                count[0] = 0

            dve.wait_ge(made, 6)
            V.tensor_copy(iota[:, :], iota_i[:, :])
            V.tensor_scalar(head_row[:, :], head_row_i[:, :], 2.0, None, ALU.mult)
            V.memset(ones[:, :], 1.0).then_inc(consts, 1)
            dve.wait_ge(weights_in, WEIGHTS)
            dve.wait_ge(setup_mm, 2)
            for g in range(2):
                V.tensor_copy(wx[:, g, D:D + 2], bank[7][:, 2 * g:2 * g + 2])
                V.tensor_copy(wsrc[:, g, :], bank[7][:, 2 * g:2 * g + 1].to_broadcast([P, P]))
            for q in range(4):
                dve.wait_ge(setup_mm, 2 + 4 * (q + 1))
                last = V.tensor_copy(pk_w[:, q * 512:(q + 1) * 512], bank[q][:, :])
            last.then_inc(setup_cp, 1)
            V.memset(top8_f[:, :, :], 0.0).then_inc(y_used, 1)
            dve.wait_ge(y_used, 1)
            dve.wait_ge(consts, 1)

            def norm(n, par):
                for t in range(NT):
                    c = mark(V.bn_stats(stats[:, t, :], xb[:, par, t, :]))
                after(c)
                for t in range(NT):
                    c = mark(V.bn_aggr(mv[:, t, :], stats[:, t, :]))
                after(c)
                V.tensor_scalar(var_e[:, :], mv[:, :, 1], EPS, None, ALU.add).then_inc(var_ready, 1)
                dve.wait_ge(std_ready, n + 1)
                c = mark(V.reciprocal(rstd[:, :], std[:, :]))
                after(c)
                dve.wait_ge(tr_ready, n + 1)
                for t in range(NT):
                    last = V.tensor_scalar(xn[:, t, :], xb[:, par, t, :], mv[:, t, 0:1], rstd[:, t:t + 1],
                                           ALU.subtract, ALU.mult)
                last.then_inc(xn_ready, 1)

            def graph(b, i, g, par):
                if g == 0:
                    dve.wait_ge(adj_in[par], 16 * (i + 1))
                c = mark(V.tensor_scalar(neg[:, :, :], adj_sb[:, par, :, :], 0.0, -NEG_BIG if g else NEG_BIG,
                                         ALU.is_equal if g else ALU.is_le, ALU.mult))
                cs = []
                for t in range(NT):
                    dve.wait_ge(z_ready, NT * (2 * b + g) + t + 1)
                    cs.append(mark(V.scalar_tensor_tensor(att[:, t, :], att[:, t, :], SLOPE, att[:, t, :],
                                                          ALU.mult, ALU.max)))
                if g == 0:
                    for t in range(NT):
                        after(max(c, cs[t]))
                        cs[t] = mark(V.tensor_tensor_reduce(
                            out=att[:, t, :], in0=att[:, t, :], in1=neg[:, t, :], scale=1.0, scalar=LOWEST,
                            op0=ALU.add, op1=ALU.max, accum_out=colmax[:, t:t + 1]))
                    for t in range(NT):
                        after(cs[t])
                        V.tensor_scalar(ncolmax[:, t:t + 1], colmax[:, t:t + 1], -1.0, None, ALU.mult)\
                            .then_inc(masked, 1)
                    dve.wait_ge(att_ready, NT * (2 * b + 1))
                    c = mark(V.reciprocal(rcol[:, :], colsum[:, :]))
                    after(c)
                    dve.wait_ge(hx_copied, 2 * b + 1)
                    for t in range(NT):
                        last = V.tensor_scalar(hx[:, t, 0:D], hx[:, t, 0:D], rcol[:, t:t + 1], None, ALU.mult)
                    last.then_inc(rhs_ready, 1)
                else:
                    for t in range(NT):
                        after(max(c, cs[t]))
                        V.tensor_tensor(att[:, t, :], att[:, t, :], neg[:, t, :], ALU.add).then_inc(masked, 1)
                    dve.wait_ge(hx_copied, 2 * b + 2)
                    V.memset(hx[:, :, D:D + 1], 1.0).then_inc(rhs_ready, 1)
                dve.wait_ge(msg_ready, 2 * b + g + 1)
                if g == 0:
                    for q in range(2):
                        c = mark(V.tensor_copy(xn[:, 2 * q:2 * q + 2, :],
                                               msg_ps[q][:, 0:2 * HX].rearrange("p (a b) -> p a b", b=HX)[:, :, 0:D]))
                else:
                    for q in range(2):
                        c = mark(V.tensor_copy(rowsum[:, 2 * q:2 * q + 2],
                                               msg_ps[q][:, 0:2 * HX].rearrange("p (a b) -> p a b", b=HX)[:, :, D]))
                    after(c)
                    c = mark(V.scalar_tensor_tensor(rowsum[:, :], rowsum[:, :], 0.0, rowsum[:, :],
                                                    ALU.is_equal, ALU.add))
                    after(c)
                    c = mark(V.reciprocal(rcol[:, :], rowsum[:, :]))
                    after(c)
                    for t in range(NT):
                        o = (t % 2) * HX
                        c = mark(V.tensor_scalar(xn[:, t, :], msg_ps[t // 2][:, o:o + D], rcol[:, t:t + 1],
                                                 None, ALU.mult))
                after(c)
                V.tensor_scalar(ex[:, :, :], xn[:, :, :], 0.0, None, ALU.min).then_inc(elu_in, 1)
                c = mark(V.scalar_tensor_tensor(xn[:, :, :], xn[:, :, :], 0.0, xb[:, par, :, :], ALU.max, ALU.add))
                after(c)
                dve.wait_ge(elu_exp, 2 * b + g + 1)
                ins = V.scalar_tensor_tensor(xb[:, par, :, :], ex[:, :, :], -1.0, xn[:, :, :], ALU.add, ALU.add)
                if g == 0:
                    after(mark(ins))
                else:
                    ins.then_inc(x3_ready, 1)
                    dve.wait_ge(x3_ready, b + 1)

            def experts(b, par):
                dve.wait_ge(gate_ready, b + 1)
                after(mark(V.tensor_copy(logits[:, :, :], gate_ps[:, 0:NT * E].rearrange("p (a b) -> p a b", b=E))))
                for t in range(NT):
                    c = mark(V.max(top8[:, t, :], logits[:, t, :]))
                after(c)
                for t in range(NT):
                    c = mark(V.max_index(top8_i[:, t, :], top8[:, t, :], logits[:, t, :]))
                after(c)
                after(mark(V.tensor_copy(top8_f[:, :, 0:2], top8_i[:, :, 0:2])))
                for t in range(NT):
                    c = mark(V.tensor_scalar(gate[:, t, :], iota[:, 0:E], top8_f[:, t, 0:1], None, ALU.is_equal))
                after(c)
                for t in range(NT):
                    c = mark(V.scalar_tensor_tensor(gate[:, t, :], iota[:, 0:E], top8_f[:, t, 1:2], gate[:, t, :],
                                                    ALU.is_equal, ALU.add))
                after(c)
                before = [0] * NT
                for e in range(E):
                    dve.wait_ge(down_ready, E * b + e + 1)
                    for t in range(NT):
                        if before[t]:
                            after(before[t])
                        before[t] = mark(V.scalar_tensor_tensor(
                            xb[:, par, t, :], down_ps[e % 2][:, t * P:(t + 1) * P], gate[:, t, e:e + 1],
                            xb[:, par, t, :], ALU.mult, ALU.add))
                    after(before[NT - 1])
                    V.memset(top8_f[:, 0, 2:3], 0.0).then_inc(down_used, 1)

            with dve.Fori(0, B // 2) as i:
                for par in range(2):
                    b = 2 * i + par
                    dve.wait_ge(x_in[par], 16 * (i + 1))
                    dve.sem_inc(turn_dve, 1)
                    norm(4 * b, par)
                    graph(b, i, 0, par)
                    norm(4 * b + 1, par)
                    experts(b, par)
                    norm(4 * b + 2, par)
                    graph(b, i, 1, par)
                    norm(4 * b + 3, par)
                    dve.wait_ge(xn_ready, 4 * b + 4)
                    V.memset(top8_f[:, 0, 2:3], 0.0).then_inc(front_done, 1)
                rewind()

            def find(H, par, t):
                n = NT * H + t
                sim = [sim_ps[t % 2][:, p * NKEY:(p + 1) * NKEY] for p in range(2)]
                dve.wait_ge(sim_ready, n + 1)
                dve.sem_inc(turn_dve, 1)
                c = [mark(V.max(half[:, 0, p, 0:8], sim[p])) for p in range(2)]
                m = [0, 0]
                for p in range(2):
                    after(c[p])
                    m[p] = mark(V.match_replace(rest[:, p, :], half[:, 0, p, 0:8], sim[p], LOWEST))
                for p in range(2):
                    ins = V.max_index(half_i[:, p, 0:8], half[:, 0, p, 0:8], sim[p])
                    if p == 1:
                        ins.then_inc(sim_used, 1)
                    else:
                        mark(ins)
                for p in range(2):
                    after(m[p])
                    c[p] = mark(V.max(half[:, 0, p, 8:16], rest[:, p, :]))
                for p in range(2):
                    after(c[p])
                    c[p] = mark(V.max_index(half_i[:, p, 8:16], half[:, 0, p, 8:16], rest[:, p, :]))
                after(c[0])
                mark(V.tensor_scalar(half[:, 1, 0, :], half_i[:, 0, :], head_row[:, ds(H % NH, 1)], None, ALU.add))
                after(c[1])
                c = mark(V.tensor_scalar(half[:, 1, 1, :], half_i[:, 1, :], float(NKEY), None, ALU.mult))
                after(c)
                o = 0
                for a, na, nb in RECTS:
                    shape = [P, 2, na, nb]
                    c = mark(V.tensor_tensor(
                        cand[:, :, o:o + na * nb].rearrange("p k (a b) -> p k a b", b=nb),
                        half[:, :, 0, a:a + na].unsqueeze(3).to_broadcast(shape),
                        half[:, :, 1, 0:nb].unsqueeze(2).to_broadcast(shape), ALU.add))
                    o += na * nb
                after(c)
                c = mark(V.max(best[:, par, t, 0:8], cand[:, 0, :]))
                after(c)
                c = mark(V.match_replace(cand2[:, :], best[:, par, t, 0:8], cand[:, 0, :], LOWEST))
                mark(V.max_index(pos_i[:, 0:8], best[:, par, t, 0:8], cand[:, 0, :]))
                mark(V.tensor_scalar(nbest[:, par, t:t + 1], best[:, par, t, 0:1], -1.0, None, ALU.mult))
                after(c)
                c = mark(V.max(best[:, par, t, 8:16], cand2[:, :]))
                after(c)
                c = mark(V.max_index(pos_i[:, 8:16], best[:, par, t, 8:16], cand2[:, :]))
                after(c)
                V.tensor_copy(pos[:, :], pos_i[:, :]).then_inc(best_ready, 1)
                dve.wait_ge(best_ready, n + 1)
                shape = [P, TOPK, NC]
                c = mark(V.tensor_tensor(pick[:, :, :], iota[:, :].unsqueeze(1).to_broadcast(shape),
                                         pos[:, :].unsqueeze(2).to_broadcast(shape), ALU.is_equal))
                after(c)
                c = mark(V.tensor_tensor(pick[:, :, :], pick[:, :, :],
                                         cand[:, 1, :].unsqueeze(1).to_broadcast(shape), ALU.mult))
                after(c)
                c = mark(V.tensor_reduce(row_f[:, :], pick[:, :, :], AX.X, ALU.add))
                after(c)
                V.tensor_copy(row_i[:, par, t, :], row_f[:, :]).then_inc(row_ready, 1)

            def weigh(H, par):
                dve.wait_ge(wexp_ready, NT * (H + 1))
                c = mark(V.reciprocal(wrec[:, :], wsum[:, par, :]))
                after(c)
                V.tensor_tensor(wgt[:, par, :, :], wexp[:, par, :, :],
                                wrec[:, :].unsqueeze(2).to_broadcast([P, NT, TOPK]), ALU.mult)\
                    .then_inc(wgt_ready, 1)

            def attend(H, par):
                def row_max(it):
                    dve.wait_ge(s_ready, NT * H + it + 1)
                    V.tensor_reduce(nrow[:, it:it + 1], s_ps[it % 2][:, 0:(it + 1) * P], AX.X, ALU.max,
                                    negate=True).then_inc(max_ready, 1)

                row_max(0)
                row_max(1)
                for it in range(NT):
                    dve.wait_ge(pT_ready, NT * H + it + 1)
                    V.tensor_copy(probT[:, 0:it + 1, it * P:(it + 1) * P],
                                  pT_ps[:, 0:(it + 1) * P].rearrange("p (a b) -> p a b", b=P))\
                        .then_inc(pT_copied, 1)
                    if it + 2 < NT:
                        row_max(it + 2)
                c = mark(V.reciprocal(prec[:, :], psum_row[:, :]))
                after(c)
                dve.wait_ge(y_in, 16 * (H // NH + 1))
                dve.wait_ge(y_ready, H + 1)
                dve.wait_ge(y_used, H + 1)
                for it in range(NT):
                    y = yb[:, ds(NT * ((H // NH) % 2) + it, 1), :].rearrange("p a b -> p (a b)")
                    last = V.scalar_tensor_tensor(y, qoy_ps[:, it * P:(it + 1) * P], prec[:, it:it + 1], y,
                                                  ALU.mult, ALU.add)
                last.then_inc(y_used, 1)

            for t in range(NT):
                find(0, 0, t)
            weigh(0, 0)

            def two_heads(i, last):
                for par in range(2):
                    H = 2 * i + par
                    if not (last and par):
                        for t in range(NT):
                            find(H + 1, 1 - par, t)
                        weigh(H + 1, 1 - par)
                    attend(H, par)
                rewind()

            rewind()
            with dve.Fori(0, HEADS // 2 - 1) as i:
                two_heads(i, False)
            two_heads(HEADS // 2 - 1, True)


def kernel(x, adj, L0_gnn_W, L0_gnn_a, L0_ffn_Wg, L0_ffn_bg, L0_ffn_W1, L0_ffn_b1, L0_ffn_W2,
           L0_ffn_b2, L1_gnn_W, L1_gnn_a, L1_ffn_Wq_pk, L1_ffn_pk_keys, L1_ffn_Wq,
           L1_ffn_keys_table, L1_ffn_values_table, L1_ffn_Wo):
    import concourse.bacc as bacc
    from concourse.bass_utils import run_bass_kernel_spmd

    def lay(a):
        return np.ascontiguousarray(a)

    a = {k: np.asarray(v) for k, v in dict(
        x=x, adj=adj, w0=L0_gnn_W, a0=L0_gnn_a, wg=L0_ffn_Wg, bg=L0_ffn_bg, w1=L0_ffn_W1, b1=L0_ffn_b1,
        w2=L0_ffn_W2, b2=L0_ffn_b2, wl=L1_gnn_W, al=L1_gnn_a, wpk=L1_ffn_Wq_pk, keys=L1_ffn_pk_keys,
        wq=L1_ffn_Wq, kt=L1_ffn_keys_table, vt=L1_ffn_values_table, wo=L1_ffn_Wo).items()}
    arrays = {
        "x_in": lay(a["x"].reshape(B * N, D)),
        "adjT": lay(a["adj"].transpose(0, 2, 1).reshape(B * N, N)),
        "wgT0": lay(a["w0"].T), "wgT1": lay(a["wl"].T),
        "wg0": lay(a["w0"]), "wg1": lay(a["wl"]),
        "ac0": lay(a["a0"].reshape(2, D).T), "ac1": lay(a["al"].reshape(2, D).T),
        "gate_w": lay(a["wg"]), "gate_b": lay(a["bg"].reshape(1, E)),
        "w1": lay(a["w1"].transpose(1, 0, 2)),
        "b1": lay(a["b1"].reshape(E, HC, P).transpose(2, 0, 1)),
        "w2": lay(a["w2"].reshape(E, HC, P, D).transpose(2, 0, 1, 3)),
        "b2": lay(a["b2"].reshape(1, E * D)),
        "wpkT": lay(a["wpk"].reshape(D, 2, NH, DK).transpose(3, 2, 1, 0).reshape(DK, NH * 2 * D)),
        "keysT": lay(a["keys"].transpose(3, 2, 0, 1).reshape(DK, NH * 2 * NKEY)),
        "wq": lay(a["wq"]),
        "table": np.concatenate([a["kt"], a["vt"]], axis=1),
        "wo": lay(a["wo"].reshape(NH, D, D).transpose(1, 0, 2).reshape(D, NH * D)),
    }
    nc = bacc.Bacc("TRN2", target_bir_lowering=False, num_devices=1)
    args = [nc.dram_tensor(k, v.shape, mybir.dt.from_np(v.dtype), kind="ExternalInput").ap()
            for k, v in arrays.items()]
    args.append(nc.dram_tensor("out", (B * N, D), F32, kind="ExternalOutput").ap())
    program(nc, *args)
    r = run_bass_kernel_spmd(nc, [arrays], core_ids=[0])
    return np.asarray(r.results[0]["out"]).reshape(B, N, D)
```

```python
from contextlib import ExitStack

import numpy as np

import concourse.bass as bass
from concourse import mybir

F32 = mybir.dt.float32
I32 = mybir.dt.int32
U32 = mybir.dt.uint32
ALU = mybir.AluOpType
ACT = mybir.ActivationFunctionType
AX = mybir.AxisListType
ds = bass.ds

P = 128
B, N, D = 16, 512, 128
NT = N // P
E, HID = 8, 256
HC = HID // P
NH, DK, NKEY = 8, 64, 128
TOPK = 16
NKV = NKEY * NKEY
RECTS = [(0, 1, 16), (1, 1, 8), (2, 2, 5), (4, 4, 3), (8, 8, 1)]
NC = sum(na * nb for _, na, nb in RECTS)
EPS = 1e-5
SLOPE = 0.2
NEG_BIG = -9000000000000000.0
CAUSAL_NEG = -1e30
LOWEST = -3.0e38
GROUP = 8
GROUPS = TOPK // GROUP
RING = NT * GROUPS
HEADS = B * NH
HX = D + 2


def program(nc, x, adjT, wgT0, wgT1, wg0, wg1, ac0, ac1, gate_w, gate_b, w1, b1, w2, b2,
            wpkT, keysT, wq, table, wo, out):
    ctx = ExitStack()
    with ctx:
        def sb(name, shape, dt=F32):
            return ctx.enter_context(nc.sbuf_tensor(name, shape, dt))

        def sem(name):
            return ctx.enter_context(nc.semaphore(name))

        ident = sb("ident", [P, P])
        causal = sb("causal", [P, P])
        iota_i = sb("iota_i", [P, NC], I32)
        iota = sb("iota", [P, NC])
        head_row_i = sb("head_row_i", [P, NH], I32)
        head_row = sb("head_row", [P, NH])
        ones = sb("ones", [1, P])
        b2_sb = sb("b2_sb", [1, E * D])
        gb_sb = sb("gb_sb", [1, E])
        gw_sb = sb("gw_sb", [P, E])
        b1_sb = sb("b1_sb", [P, E, HC])
        w1_sb = sb("w1_sb", [P, E, HID])
        w2_sb = sb("w2_sb", [P, E, HC, D])
        ac_sb = sb("ac_sb", [P, 2, 2])
        wx = sb("wx", [P, 2, HX])
        wsrc = sb("wsrc", [P, 2, P])
        pk_w = sb("pk_w", [P, NH * 2 * NKEY])
        wq_sb = sb("wq_sb", [P, NH * D])
        wo_sb = sb("wo_sb", [P, NH * D])

        xb = sb("xb", [P, NT, D])
        adj_sb = sb("adj_sb", [P, NT, N], I32)
        neg = sb("neg", [P, NT, N])
        att = sb("att", [P, NT, N])
        xn = sb("xn", [P, NT, D])
        xT = sb("xT", [P, N])
        hx = sb("hx", [P, NT, HX])
        hid = sb("hid", [P, 4, N])
        ex = sb("ex", [P, NT, D])
        stats = sb("stats", [P, NT, 6])
        mv = sb("mv", [P, NT, 2])
        var_e = sb("var_e", [P, NT])
        std = sb("std", [P, NT])
        rstd = sb("rstd", [P, NT])
        colmax = sb("colmax", [P, NT])
        ncolmax = sb("ncolmax", [P, NT])
        colsum = sb("colsum", [P, NT])
        rcol = sb("rcol", [P, NT])
        rowsum = sb("rowsum", [P, NT])
        logits = sb("logits", [P, NT, E])
        top8 = sb("top8", [P, NT, 8])
        top8_i = sb("top8_i", [P, NT, 8], U32)
        top8_f = sb("top8_f", [P, NT, 8])
        gate = sb("gate", [P, NT, E])
        mark_cell = sb("mark_cell", [P, 1])

        xs = sb("xs", [P, N])
        qT = sb("qT", [P, 2, N])
        kv = sb("kv", [P, 2, NT, 2 * D])
        rows = sb("rows", [P, RING * GROUP, 2 * D])
        diag = sb("diag", [P, TOPK, P])
        prob = sb("prob", [P, 2, N])
        probT = sb("probT", [P, NT, N])
        oT = sb("oT", [P, N])
        yb = sb("yb", [P, NT, D])
        half = sb("half", [P, 2, 2, TOPK])
        half_i = sb("half_i", [P, 2, TOPK], U32)
        rest = sb("rest", [P, 2, NKEY])
        cand = sb("cand", [P, 2, NC])
        cand2 = sb("cand2", [P, NC])
        best = sb("best", [P, 2, NT, TOPK])
        nbest = sb("nbest", [P, 2, NT])
        pos_i = sb("pos_i", [P, TOPK], U32)
        pos = sb("pos", [P, TOPK])
        pick = sb("pick", [P, TOPK, NC])
        row_f = sb("row_f", [P, TOPK])
        row_i = sb("row_i", [P, 2, NT, TOPK], U32)
        wexp = sb("wexp", [P, 2, NT, TOPK])
        wsum = sb("wsum", [P, 2, NT])
        wrec = sb("wrec", [P, NT])
        wgt = sb("wgt", [P, 2, NT, TOPK])
        nrow = sb("nrow", [P, NT])
        psum_row = sb("psum_row", [P, NT])
        prec = sb("prec", [P, NT])

        wpkT_sb = rows[0:DK, 0:8, :].rearrange("p a b -> p (a b)")
        keysT_sb = rows[0:DK, 8:16, :].rearrange("p a b -> p (a b)")
        wgT_sb = [rows[:, 16 + g, 0:D] for g in range(2)]

        bank = [ctx.enter_context(nc.psum_tensor(f"bank{i}", [P, 512], F32)) for i in range(8)]
        sim_ps = bank[0]
        hx_ps = msg_ps = up_ps = [bank[1], bank[2]]
        gate_ps = bank[1]
        kv_ps = bank[3]
        s_ps = down_ps = [bank[4], bank[5]]
        src_ps = bank[4]
        pT_ps = tr_ps = bank[6]
        qoy_ps = bank[7]

        turn_pool, turn_dve, turn_sp = sem("turn_pool"), sem("turn_dve"), sem("turn_sp")
        weights_in = sem("weights_in")
        made = sem("made")
        setup_mm, setup_cp = sem("setup_mm"), sem("setup_cp")
        chain = sem("chain")
        x_in, adj_in = sem("x_in"), sem("adj_in")
        var_ready, std_ready, xn_ready = sem("var_ready"), sem("std_ready"), sem("xn_ready")
        tr_ready, xT_ready = sem("tr_ready"), sem("xT_ready")
        src_ready, hx_ready, hx_copied = sem("src_ready"), sem("hx_ready"), sem("hx_copied")
        z_ready, masked, att_ready = sem("z_ready"), sem("masked"), sem("att_ready")
        rhs_ready, msg_ready = sem("rhs_ready"), sem("msg_ready")
        elu_in, elu_exp = sem("elu_in"), sem("elu_exp")
        gate_ready, gate_copied = sem("gate_ready"), sem("gate_copied")
        up_ready, gelu_done = sem("up_ready"), sem("gelu_done")
        down_ready, down_used = sem("down_ready"), sem("down_used")
        adj_used, xb_moved = sem("adj_used"), sem("xb_moved")
        y_out = sem("y_out")
        q_in, q_ready, q_copied = sem("q_in"), sem("q_ready"), sem("q_copied")
        sim_ready, sim_used = sem("sim_ready"), sem("sim_used")
        best_ready, wexp_ready, wgt_ready = sem("best_ready"), sem("wexp_ready"), sem("wgt_ready")
        row_ready = sem("row_ready")
        row_in = [sem(f"row_in{i}") for i in range(RING)]
        diag_ready, kv_group, kv_copied = sem("diag_ready"), sem("kv_group"), sem("kv_copied")
        s_ready, max_ready, p_ready = sem("s_ready"), sem("max_ready"), sem("p_ready")
        pT_ready, pT_copied = sem("pT_ready"), sem("pT_copied")
        o_ready, o_copied, y_ready, y_used = sem("o_ready"), sem("o_copied"), sem("y_ready"), sem("y_used")


        x_v = x.rearrange("(n p) d -> p n d", p=P)
        adj_v = adjT.rearrange("(n p) i -> p n i", p=P)
        out_v = out.rearrange("(n p) d -> p n d", p=P)

        weight_loads = [
            (ac_sb[:, 0, :], ac0), (ac_sb[:, 1, :], ac1), (wgT_sb[0], wgT0), (wgT_sb[1], wgT1),
            (wx[:, 0, 0:D], wg0), (wx[:, 1, 0:D], wg1), (gw_sb[:, :], gate_w), (gb_sb[:, :], gate_b),
            (b1_sb[:, :, :], b1), (b2_sb[:, :], b2), (wpkT_sb, wpkT), (keysT_sb, keysT),
            (w1_sb[:, :, :], w1), (w2_sb[:, :, :, :], w2), (wq_sb[:, :], wq), (wo_sb[:, :], wo),
        ]
        WEIGHTS = 16 * len(weight_loads)

        block = ctx.enter_context(nc.Block())

        NORM0, GRAPH0, NORM1, GATE, UP, NORM2, GRAPH1, NORM3 = 0, 1, 4, 5, 6, 15, 16, 19
        STEPS = 20
        FIRST_UNIT = 2

        def step_of(h, t):
            step = NT * h + t - FIRST_UNIT
            return step if 0 <= step < STEPS else None

        @block.sync
        def _(sp):
            sp.sem_inc(y_out, 1)
            sp.dma_start(xb[:, :, :], x_v[:, 0:NT, :]).then_inc(x_in, 16)
            for dst, src in weight_loads:
                sp.dma_start(dst, src).then_inc(weights_in, 16)
            sp.dma_start(adj_sb[:, :, :], adj_v[:, 0:NT, :]).then_inc(adj_in, 16)

            def load_front(f):
                sp.wait_ge(adj_used, f)
                sp.sem_inc(turn_sp, 1)
                sp.dma_start(adj_sb[:, :, :], adj_v[:, ds(NT * f, NT), :]).then_inc(adj_in, 16)
                sp.wait_ge(xb_moved, f)
                sp.sem_inc(turn_sp, 1)
                sp.dma_start(xb[:, :, :], x_v[:, ds(NT * f, NT), :]).then_inc(x_in, 16)

            def store_y(b):
                sp.wait_ge(y_used, NH * (b + 1) + 1)
                sp.sem_inc(turn_sp, 1)
                sp.dma_start(out_v[:, ds(NT * b, NT), :], yb[:, :, :]).then_inc(y_out, 16)
                sp.wait_ge(y_out, 16 * (b + 1) + 1)
                sp.sem_inc(turn_sp, 1)

            with sp.Fori(0, B - 1) as b:
                load_front(b + 1)
                store_y(b)
            store_y(B - 1)

        @block.gpsimd
        def _(pool):
            pool.memset(ident[:, :], 0.0).then_inc(made, 1)
            pool.memset(causal[:, :], 0.0).then_inc(made, 1)
            pool.wait_ge(made, 2)
            pool.affine_select(out=ident[:, :], in_=ident[:, :], compare_op=ALU.not_equal, fill=1.0,
                               base=0, pattern=[[-1, P]], channel_multiplier=1).then_inc(made, 1)
            pool.affine_select(out=causal[:, :], in_=causal[:, :], compare_op=ALU.is_ge, fill=CAUSAL_NEG,
                               base=0, pattern=[[-1, P]], channel_multiplier=1).then_inc(made, 1)
            pool.iota(iota_i[:, :], [[1, NC]], base=0, channel_multiplier=0).then_inc(made, 1)
            pool.iota(head_row_i[:, :], [[NKV, NH]], base=0, channel_multiplier=0).then_inc(made, 1)
            pool.wait_ge(made, 6)

            with pool.Fori(0, HEADS // 2) as i:
                for par in range(2):
                    H = 2 * i + par
                    for t in range(NT):
                        pool.wait_ge(row_ready, NT * H + t + 1)
                        for g in range(GROUPS):
                            ring = GROUPS * t + g
                            pool.wait_ge(kv_group, GROUPS * (NT * H + t) + g + 1)
                            pool.sem_inc(turn_pool, 1)
                            for k in range(GROUP):
                                pool.indirect_dma_start(
                                    rows[:, GROUP * ring + k, :], None, table,
                                    bass.IndirectOffsetOnAxis(
                                        ap=row_i[:, par, t, GROUP * g + k:GROUP * g + k + 1], axis=0),
                                ).then_inc(row_in[ring], 16)

        @block.tensor
        def _(pe):
            mm = nc.tensor.matmul
            pe.wait_ge(weights_in, WEIGHTS)
            for g in range(2):
                mm(bank[7][:, 2 * g:2 * g + 2], wgT_sb[g], ac_sb[:, g, :], start=True, stop=True)\
                    .then_inc(setup_mm, 1)
            for c in range(NH * 2):
                mm(bank[c // 4][:, (c % 4) * P:(c % 4 + 1) * P], wpkT_sb[:, c * P:(c + 1) * P],
                   keysT_sb[:, c * P:(c + 1) * P], start=True, stop=True).then_inc(setup_mm, 1)
            pe.sem_inc(kv_group, RING)
            pe.sem_inc(tr_ready, 1)
            pe.wait_ge(setup_cp, 1)
            pe.wait_ge(made, 6)

            def transposed(n):
                pe.wait_ge(xn_ready, n + 1)
                for t in range(NT):
                    last = nc.tensor.transpose(tr_ps[:, t * P:(t + 1) * P], xn[:, t, :], ident[:, :])
                last.then_inc(tr_ready, 1)
                pe.wait_ge(xT_ready, n + 2)

            def project(f, g):
                pe.wait_ge(xT_ready, 4 * f + 2 * g + 2)
                mm(src_ps[:, :], wsrc[:, g, :], xT[:, :], start=True, stop=True).then_inc(src_ready, 1)
                for t in range(NT):
                    last = mm(hx_ps[t // 2][:, (t % 2) * HX:(t % 2 + 1) * HX], xT[:, t * P:(t + 1) * P],
                              wx[:, g, :], start=True, stop=True)
                last.then_inc(hx_ready, 1)

            def messages(f, g):
                width = D + g
                pe.wait_ge(rhs_ready, 2 * f + g + 1)
                pe.wait_ge(att_ready, NT * (2 * f + g + 1))
                for it in range(NT):
                    for jt in range(NT):
                        last = mm(msg_ps[it // 2][:, (it % 2) * HX:(it % 2) * HX + width],
                                  att[:, jt, it * P:(it + 1) * P], hx[:, jt, 0:width],
                                  start=(jt == 0), stop=(jt == NT - 1))
                last.then_inc(msg_ready, 1)

            def gates(f):
                pe.wait_ge(xT_ready, 4 * f + 3)
                for t in range(NT):
                    o = gate_ps[:, t * E:(t + 1) * E]
                    mm(o, xT[:, t * P:(t + 1) * P], gw_sb[:, :], start=True, stop=False)
                    last = mm(o, ones[:, :], gb_sb[:, :], start=False, stop=True)
                last.then_inc(gate_ready, 1)

            def up(f, e):
                if e == 0:
                    pe.wait_ge(gate_copied, f + 1)
                else:
                    pe.wait_ge(gelu_done, HC * (E * f + e))
                for c in range(HC):
                    mm(up_ps[c][:, :], w1_sb[:, e, c * P:(c + 1) * P], xT[:, :],
                       start=True, stop=True).then_inc(up_ready, 1)

            def down(f, e):
                pe.wait_ge(gelu_done, HC * (E * f + e + 1))
                for t in range(NT):
                    o = down_ps[e % 2][:, t * P:(t + 1) * P]
                    for c in range(HC):
                        mm(o, hid[:, (HC * e + c) % 4, t * P:(t + 1) * P], w2_sb[:, e, c, :],
                           start=(c == 0), stop=False)
                    last = mm(o, ones[:, :], b2_sb[:, e * D:(e + 1) * D], start=False, stop=True)
                last.then_inc(down_ready, 1)

            def early(f, step):
                if step in (GRAPH0, GRAPH1):
                    project(f, int(step == GRAPH1))
                if step == GATE:
                    gates(f)
                if UP + 1 <= step <= UP + E:
                    down(f, step - UP - 1)
                if UP <= step < UP + E:
                    up(f, step - UP)

            def late(f, step):
                if step in (NORM0, NORM1, NORM2, NORM3):
                    transposed(4 * f + (NORM0, NORM1, NORM2, NORM3).index(step))
                if step in (GRAPH0, GRAPH1):
                    pe.wait_ge(z_ready, NT * (2 * f + int(step == GRAPH1) + 1))
                if step in (GRAPH0 + 1, GRAPH1 + 1):
                    messages(f, int(step == GRAPH1 + 1))
                if UP + 1 <= step <= UP + E:
                    pe.wait_ge(down_used, E * f + step - UP)

            def query(H, h, first=False):
                pe.wait_ge(q_in, H // NH + 1 if first else (H + NH - h) // NH)
                if not first:
                    pe.wait_ge(y_used, H)
                mm(qoy_ps[:, :], wq_sb[:, h * D:(h + 1) * D], xs[:, :], start=True, stop=True)\
                    .then_inc(q_ready, 1)

            def scores(H, h, t, first=False):
                if not first:
                    pe.wait_ge(sim_used, NT * H + t)
                elif t:
                    pe.wait_ge(sim_used, t)
                mm(sim_ps[:, 0:2 * NKEY], xs[:, t * P:(t + 1) * P],
                   pk_w[:, h * 2 * NKEY:(h + 1) * 2 * NKEY], start=True, stop=True).then_inc(sim_ready, 1)

            def combine(H, par, t):
                n = NT * H + t
                pe.wait_ge(kv_copied, n + 1)
                for k in range(TOPK):
                    slot = TOPK * t + k
                    if k % GROUP == 0:
                        pe.wait_ge(diag_ready, GROUPS * n + k // GROUP + 1)
                        pe.wait_ge(row_in[slot // GROUP], 16 * GROUP * (H + 1))
                    mm(kv_ps[:, 0:P], rows[:, slot, 0:D], diag[:, k, :], start=(k == 0),
                       stop=(k == TOPK - 1), skip_group_check=True)
                    last = mm(kv_ps[:, P:P + D], diag[:, k, :], rows[:, slot, D:2 * D], start=False,
                              stop=(k == TOPK - 1), skip_group_check=True)
                    if k % GROUP == GROUP - 1:
                        last.then_inc(kv_group, 1)

            def attend(H, h, par, last_head):
                pe.wait_ge(kv_copied, NT * (H + 1) + 1)

                def s_tile(it):
                    if it >= 2:
                        pe.wait_ge(p_ready, NT * H + it - 1)
                    q = qT[:, par, it * P:(it + 1) * P]
                    if it:
                        mm(s_ps[it % 2][:, 0:it * P].rearrange("p (a b) -> p a b", b=P), q,
                           kv[:, par, 0:it, 0:P], start=True, stop=True)
                    o = s_ps[it % 2][:, it * P:(it + 1) * P]
                    mm(o, q, kv[:, par, it, 0:P], start=True, stop=False)
                    mm(o, ident[:, :], causal[:, :], start=False, stop=True).then_inc(s_ready, 1)

                def t_tile(it):
                    pe.wait_ge(p_ready, NT * H + it + 1)
                    if it:
                        pe.wait_ge(pT_copied, NT * H + it)
                    for jt in range(it + 1):
                        last = nc.tensor.transpose(pT_ps[:, jt * P:(jt + 1) * P],
                                                   prob[:, it % 2, jt * P:(jt + 1) * P], ident[:, :])
                    last.then_inc(pT_ready, 1)

                s_tile(0)
                s_tile(1)
                for it in range(NT):
                    t_tile(it)
                    if it + 2 < NT:
                        s_tile(it + 2)
                if not last_head:
                    pe.wait_ge(q_copied, H + 2)
                pe.wait_ge(pT_copied, NT * (H + 1))
                for it in range(NT):
                    for jt in range(it + 1):
                        last = mm(qoy_ps[:, it * P:(it + 1) * P], kv[:, par, jt, D:2 * D],
                                  probT[:, jt, it * P:(it + 1) * P], start=(jt == 0), stop=(jt == it))
                last.then_inc(o_ready, 1)
                pe.wait_ge(o_copied, H + 1)
                for it in range(NT):
                    last = mm(qoy_ps[:, it * P:(it + 1) * P], oT[:, it * P:(it + 1) * P],
                              wo_sb[:, h * D:(h + 1) * D], start=True, stop=True)
                last.then_inc(y_ready, 1)

            for step in range(STEPS):
                early(0, step)
                late(0, step)
            query(0, 0, first=True)
            for t in range(NT):
                scores(0, 0, t, first=True)
            pe.wait_ge(q_copied, 1)

            def batch(b, last):
                for h in range(NH):
                    H = NH * b + h
                    more = not (last and h == NH - 1)
                    if more:
                        query(H + 1, (h + 1) % NH)
                    for t in range(NT):
                        step = None if last else step_of(h, t)
                        if step is not None:
                            early(b + 1, step)
                        if more:
                            scores(H + 1, (h + 1) % NH, t)
                        combine(H, h % 2, t)
                        if step is not None:
                            late(b + 1, step)
                    attend(H, h, h % 2, not more)

            with pe.Fori(0, B - 1) as b:
                batch(b, False)
            batch(B - 1, True)

        @block.scalar
        def _(act):
            A = nc.scalar.activation
            act.sem_inc(kv_copied, 1)
            act.sem_inc(xT_ready, 1)
            act.wait_ge(weights_in, WEIGHTS)

            def std_dev(n):
                act.wait_ge(var_ready, n + 1)
                A(std[:, :], var_e[:, :], ACT.Sqrt).then_inc(std_ready, 1)

            def copy_xT(n):
                act.wait_ge(tr_ready, n + 2)
                A(xT[:, :], tr_ps[:, :], ACT.Copy).then_inc(xT_ready, 1)

            def pair_scores(f, g):
                act.wait_ge(hx_ready, 2 * f + g + 1)
                for q in range(2):
                    last = A(hx[:, 2 * q:2 * q + 2, :].rearrange("p a b -> p (a b)"),
                             hx_ps[q][:, 0:2 * HX], ACT.Copy)
                last.then_inc(hx_copied, 1)
                act.wait_ge(hx_copied, 2 * f + g + 1)
                for t in range(NT):
                    A(att[:, t, :], src_ps[:, :], ACT.Identity, bias=hx[:, t, D + 1:D + 2])\
                        .then_inc(z_ready, 1)

            def pair_weights(f, g):
                for t in range(NT):
                    act.wait_ge(masked, NT * (2 * f + g) + t + 1)
                    if g == 0:
                        A(att[:, t, :], att[:, t, :], ACT.Exp, bias=ncolmax[:, t:t + 1],
                          accum_out=colsum[:, t:t + 1]).then_inc(att_ready, 1)
                    else:
                        A(att[:, t, :], att[:, t, :], ACT.Exp, scale=-1.0).then_inc(att_ready, 1)

            def elu(f, g):
                act.wait_ge(elu_in, 2 * f + g + 1)
                A(ex[:, :, :], ex[:, :, :], ACT.Exp).then_inc(elu_exp, 1)

            def gelu(f, e):
                for c in range(HC):
                    u = HC * e + c
                    act.wait_ge(up_ready, HC * E * f + u + 1)
                    if e >= 2:
                        act.wait_ge(down_ready, E * f + e - 1)
                    A(hid[:, u % 4, :], up_ps[c][:, :], ACT.Gelu, bias=b1_sb[:, e, c:c + 1])\
                        .then_inc(gelu_done, 1)

            def early(f, step):
                if step in (NORM0, NORM1, NORM2, NORM3):
                    std_dev(4 * f + (NORM0, NORM1, NORM2, NORM3).index(step))
                if step in (GRAPH0, GRAPH1):
                    pair_scores(f, int(step == GRAPH1))
                if UP <= step < UP + E:
                    gelu(f, step - UP)
                if step in (GRAPH0 + 1, GRAPH1 + 1):
                    pair_weights(f, int(step == GRAPH1 + 1))

            def late(f, step):
                if step in (NORM0, NORM1, NORM2, NORM3):
                    copy_xT(4 * f + (NORM0, NORM1, NORM2, NORM3).index(step))
                if step in (GRAPH0 + 2, GRAPH1 + 2):
                    elu(f, int(step == GRAPH1 + 2))

            def next_batch(f):
                act.wait_ge(xT_ready, 4 * f + 5)
                A(xs[:, :], xT[:, :], ACT.Copy).then_inc(q_in, 1)

            def query(H, par):
                act.wait_ge(q_ready, H + 1)
                A(qT[:, par, :], qoy_ps[:, :], ACT.Copy, scale=float(D) ** -0.5).then_inc(q_copied, 1)

            def best_exp(H, par, t):
                act.wait_ge(best_ready, NT * H + t + 1)
                A(wexp[:, par, t, :], best[:, par, t, :], ACT.Exp, bias=nbest[:, par, t:t + 1],
                  accum_out=wsum[:, par, t:t + 1]).then_inc(wexp_ready, 1)

            def diagonals(H, par, t):
                n = NT * H + t
                if t == 0:
                    act.wait_ge(wgt_ready, H + 1)
                for k in range(TOPK):
                    if k % GROUP == 0:
                        act.wait_ge(kv_group, GROUPS * (n - 1) + k // GROUP + 1 + RING)
                    last = A(diag[:, k, :], ident[:, :], ACT.Copy, scale=wgt[:, par, t, k:k + 1])
                    if k % GROUP == GROUP - 1:
                        last.then_inc(diag_ready, 1)

            def copy_kv(H, par, t):
                act.wait_ge(kv_group, GROUPS * (NT * H + t + 1) + RING)
                A(kv[:, par, t, :], kv_ps[:, 0:2 * D], ACT.Copy).then_inc(kv_copied, 1)

            def attend(H, par):
                for it in range(NT):
                    act.wait_ge(max_ready, NT * H + it + 1)
                    if it >= 2:
                        act.wait_ge(pT_ready, NT * H + it - 1)
                    w = (it + 1) * P
                    A(prob[:, it % 2, 0:w], s_ps[it % 2][:, 0:w], ACT.Exp, bias=nrow[:, it:it + 1],
                      accum_out=psum_row[:, it:it + 1]).then_inc(p_ready, 1)
                act.wait_ge(o_ready, H + 1)
                A(oT[:, :], qoy_ps[:, :], ACT.Copy).then_inc(o_copied, 1)

            for step in range(STEPS):
                early(0, step)
                late(0, step)
            next_batch(0)
            query(0, 0)
            for t in range(NT):
                best_exp(0, 0, t)

            def batch(b, last):
                for h in range(NH):
                    H = NH * b + h
                    more = not (last and h == NH - 1)
                    if more:
                        if h == NH - 1:
                            next_batch(b + 1)
                        query(H + 1, (h + 1) % 2)
                    for t in range(NT):
                        step = None if last else step_of(h, t)
                        if step is not None:
                            early(b + 1, step)
                        diagonals(H, h % 2, t)
                        copy_kv(H, h % 2, t)
                        if more:
                            best_exp(H + 1, (h + 1) % 2, t)
                        if step is not None:
                            late(b + 1, step)
                    attend(H, h % 2)

            with act.Fori(0, B - 1) as b:
                batch(b, False)
            batch(B - 1, True)

        @block.vector
        def _(dve):
            V = nc.vector
            count = [0]

            def mark(ins):
                count[0] += 1
                ins.then_inc(chain, 1)
                return count[0]

            def after(value):
                dve.wait_ge(chain, value)

            def rewind():
                after(count[0])
                dve.sem_clear(chain)
                count[0] = 0

            dve.wait_ge(made, 6)
            V.tensor_copy(iota[:, :], iota_i[:, :])
            V.tensor_copy(head_row[:, :], head_row_i[:, :])
            V.memset(ones[:, :], 1.0)
            dve.wait_ge(setup_mm, 2)
            for g in range(2):
                V.tensor_copy(wx[:, g, D:D + 2], bank[7][:, 2 * g:2 * g + 2])
                V.tensor_copy(wsrc[:, g, :], bank[7][:, 2 * g:2 * g + 1].to_broadcast([P, P]))
            for q in range(4):
                dve.wait_ge(setup_mm, 2 + 4 * (q + 1))
                last = V.tensor_copy(pk_w[:, q * 512:(q + 1) * 512], bank[q][:, :])
            last.then_inc(setup_cp, 1)
            V.memset(mark_cell[:, :], 0.0).then_inc(y_used, 1)
            dve.wait_ge(y_used, 1)

            def statistics(f, n):
                if n == 0:
                    dve.wait_ge(x_in, 16 * (f + 1))
                    dve.sem_inc(turn_dve, 1)
                for t in range(NT):
                    c = mark(V.bn_stats(stats[:, t, :], xb[:, t, :]))
                after(c)
                for t in range(NT):
                    c = mark(V.bn_aggr(mv[:, t, :], stats[:, t, :]))
                after(c)
                V.tensor_scalar(var_e[:, :], mv[:, :, 1], EPS, None, ALU.add).then_inc(var_ready, 1)

            def normalise(f, n):
                dve.wait_ge(std_ready, 4 * f + n + 1)
                c = mark(V.reciprocal(rstd[:, :], std[:, :]))
                after(c)
                dve.wait_ge(tr_ready, 4 * f + n + 1)
                for t in range(NT):
                    last = V.tensor_scalar(xn[:, t, :], xb[:, t, :], mv[:, t, 0:1], rstd[:, t:t + 1],
                                           ALU.subtract, ALU.mult)
                last.then_inc(xn_ready, 1)

            def mask_pairs(f, g):
                if g == 0:
                    dve.wait_ge(adj_in, 16 * (f + 1))
                c = mark(V.tensor_scalar(neg[:, :, :], adj_sb[:, :, :], 0.0, -NEG_BIG if g else NEG_BIG,
                                         ALU.is_equal if g else ALU.is_le, ALU.mult))
                cs = []
                for t in range(NT):
                    dve.wait_ge(z_ready, NT * (2 * f + g) + t + 1)
                    cs.append(mark(V.scalar_tensor_tensor(att[:, t, :], att[:, t, :], SLOPE, att[:, t, :],
                                                          ALU.mult, ALU.max)))
                if g == 0:
                    for t in range(NT):
                        after(max(c, cs[t]))
                        cs[t] = mark(V.tensor_tensor_reduce(
                            out=att[:, t, :], in0=att[:, t, :], in1=neg[:, t, :], scale=1.0, scalar=LOWEST,
                            op0=ALU.add, op1=ALU.max, accum_out=colmax[:, t:t + 1]))
                    for t in range(NT):
                        after(cs[t])
                        V.tensor_scalar(ncolmax[:, t:t + 1], colmax[:, t:t + 1], -1.0, None, ALU.mult)\
                            .then_inc(masked, 1)
                else:
                    for t in range(NT):
                        after(max(c, cs[t]))
                        V.tensor_tensor(att[:, t, :], att[:, t, :], neg[:, t, :], ALU.add).then_inc(masked, 1)
                    V.memset(mark_cell[:, :], 0.0).then_inc(adj_used, 1)

            def right_side(f, g):
                if g == 0:
                    dve.wait_ge(att_ready, NT * (2 * f + 1))
                    c = mark(V.reciprocal(rcol[:, :], colsum[:, :]))
                    after(c)
                    dve.wait_ge(hx_copied, 2 * f + 1)
                    for t in range(NT):
                        last = V.tensor_scalar(hx[:, t, 0:D], hx[:, t, 0:D], rcol[:, t:t + 1], None, ALU.mult)
                    last.then_inc(rhs_ready, 1)
                else:
                    dve.wait_ge(hx_copied, 2 * f + 2)
                    V.memset(hx[:, :, D:D + 1], 1.0).then_inc(rhs_ready, 1)

            def received(f, g):
                dve.wait_ge(msg_ready, 2 * f + g + 1)
                msg = [msg_ps[q][:, 0:2 * HX].rearrange("p (a b) -> p a b", b=HX) for q in range(2)]
                if g == 0:
                    for q in range(2):
                        c = mark(V.tensor_copy(xn[:, 2 * q:2 * q + 2, :], msg[q][:, :, 0:D]))
                else:
                    for q in range(2):
                        c = mark(V.tensor_copy(rowsum[:, 2 * q:2 * q + 2], msg[q][:, :, D]))
                    after(c)
                    c = mark(V.scalar_tensor_tensor(rowsum[:, :], rowsum[:, :], 0.0, rowsum[:, :],
                                                    ALU.is_equal, ALU.add))
                    after(c)
                    c = mark(V.reciprocal(rcol[:, :], rowsum[:, :]))
                    after(c)
                    for t in range(NT):
                        c = mark(V.tensor_scalar(xn[:, t, :], msg[t // 2][:, t % 2, 0:D], rcol[:, t:t + 1],
                                                 None, ALU.mult))
                after(c)
                V.tensor_scalar(ex[:, :, :], xn[:, :, :], 0.0, None, ALU.min).then_inc(elu_in, 1)
                after(mark(V.scalar_tensor_tensor(xn[:, :, :], xn[:, :, :], 0.0, xb[:, :, :], ALU.max, ALU.add)))

            def elu(f, g):
                dve.wait_ge(elu_exp, 2 * f + g + 1)
                after(mark(V.scalar_tensor_tensor(xb[:, :, :], ex[:, :, :], -1.0, xn[:, :, :], ALU.add, ALU.add)))

            def choose(f):
                dve.wait_ge(gate_ready, f + 1)
                V.tensor_copy(logits[:, :, :], gate_ps[:, 0:NT * E].rearrange("p (a b) -> p a b", b=E))\
                    .then_inc(gate_copied, 1)
                dve.wait_ge(gate_copied, f + 1)
                dve.sem_inc(turn_dve, 1)
                for t in range(NT):
                    c = mark(V.max(top8[:, t, :], logits[:, t, :]))
                after(c)
                for t in range(NT):
                    c = mark(V.max_index(top8_i[:, t, :], top8[:, t, :], logits[:, t, :]))
                after(c)
                after(mark(V.tensor_copy(top8_f[:, :, 0:2], top8_i[:, :, 0:2])))
                for t in range(NT):
                    c = mark(V.tensor_scalar(gate[:, t, :], iota[:, 0:E], top8_f[:, t, 0:1], None, ALU.is_equal))
                after(c)
                for t in range(NT):
                    c = mark(V.scalar_tensor_tensor(gate[:, t, :], iota[:, 0:E], top8_f[:, t, 1:2], gate[:, t, :],
                                                    ALU.is_equal, ALU.add))
                after(c)

            def add_expert(f, e):
                dve.wait_ge(down_ready, E * f + e + 1)
                for t in range(NT):
                    c = mark(V.scalar_tensor_tensor(
                        xb[:, t, :], down_ps[e % 2][:, t * P:(t + 1) * P], gate[:, t, e:e + 1],
                        xb[:, t, :], ALU.mult, ALU.add))
                after(c)
                V.memset(mark_cell[:, :], 0.0).then_inc(down_used, 1)

            def early(f, step):
                if step in (NORM0, NORM1, NORM2, NORM3):
                    statistics(f, (NORM0, NORM1, NORM2, NORM3).index(step))
                if step in (GRAPH0 + 2, GRAPH1 + 2):
                    received(f, int(step == GRAPH1 + 2))

            def late(f, step):
                if step in (NORM0, NORM1, NORM2, NORM3):
                    normalise(f, (NORM0, NORM1, NORM2, NORM3).index(step))
                if step in (GRAPH0, GRAPH1):
                    mask_pairs(f, int(step == GRAPH1))
                if step in (GRAPH0 + 1, GRAPH1 + 1):
                    right_side(f, int(step == GRAPH1 + 1))
                if step in (GRAPH0 + 2, GRAPH1 + 2):
                    elu(f, int(step == GRAPH1 + 2))
                if step == GATE:
                    choose(f)
                if UP + 1 <= step <= UP + E:
                    add_expert(f, step - UP - 1)

            def move_stream(f):
                dve.wait_ge(y_out, 16 * f + 1)
                V.tensor_copy(yb[:, :, :], xb[:, :, :]).then_inc(xb_moved, 1)

            def find(H, h, par, t):
                n = NT * H + t
                sim = [sim_ps[:, p * NKEY:(p + 1) * NKEY] for p in range(2)]
                dve.wait_ge(sim_ready, n + 1)
                dve.sem_inc(turn_dve, 1)
                c = [mark(V.max(half[:, 0, p, 0:8], sim[p])) for p in range(2)]
                m = [0, 0]
                for p in range(2):
                    after(c[p])
                    m[p] = mark(V.match_replace(rest[:, p, :], half[:, 0, p, 0:8], sim[p], LOWEST))
                for p in range(2):
                    ins = V.max_index(half_i[:, p, 0:8], half[:, 0, p, 0:8], sim[p])
                    if p == 1:
                        ins.then_inc(sim_used, 1)
                    else:
                        mark(ins)
                for p in range(2):
                    after(m[p])
                    c[p] = mark(V.max(half[:, 0, p, 8:16], rest[:, p, :]))
                for p in range(2):
                    after(c[p])
                    c[p] = mark(V.max_index(half_i[:, p, 8:16], half[:, 0, p, 8:16], rest[:, p, :]))
                after(c[0])
                mark(V.tensor_scalar(half[:, 1, 0, :], half_i[:, 0, :], head_row[:, h:h + 1], None, ALU.add))
                after(c[1])
                c = mark(V.tensor_scalar(half[:, 1, 1, :], half_i[:, 1, :], float(NKEY), None, ALU.mult))
                after(c)
                o = 0
                for a, na, nb in RECTS:
                    shape = [P, 2, na, nb]
                    c = mark(V.tensor_tensor(
                        cand[:, :, o:o + na * nb].rearrange("p k (a b) -> p k a b", b=nb),
                        half[:, :, 0, a:a + na].unsqueeze(3).to_broadcast(shape),
                        half[:, :, 1, 0:nb].unsqueeze(2).to_broadcast(shape), ALU.add))
                    o += na * nb
                after(c)
                c = mark(V.max(best[:, par, t, 0:8], cand[:, 0, :]))
                after(c)
                c = mark(V.match_replace(cand2[:, :], best[:, par, t, 0:8], cand[:, 0, :], LOWEST))
                mark(V.max_index(pos_i[:, 0:8], best[:, par, t, 0:8], cand[:, 0, :]))
                mark(V.tensor_scalar(nbest[:, par, t:t + 1], best[:, par, t, 0:1], -1.0, None, ALU.mult))
                after(c)
                c = mark(V.max(best[:, par, t, 8:16], cand2[:, :]))
                after(c)
                c = mark(V.max_index(pos_i[:, 8:16], best[:, par, t, 8:16], cand2[:, :]))
                after(c)
                V.tensor_copy(pos[:, :], pos_i[:, :]).then_inc(best_ready, 1)
                dve.wait_ge(best_ready, n + 1)
                shape = [P, TOPK, NC]
                c = mark(V.tensor_tensor(pick[:, :, :], iota[:, :].unsqueeze(1).to_broadcast(shape),
                                         pos[:, :].unsqueeze(2).to_broadcast(shape), ALU.is_equal))
                after(c)
                c = mark(V.tensor_tensor(pick[:, :, :], pick[:, :, :],
                                         cand[:, 1, :].unsqueeze(1).to_broadcast(shape), ALU.mult))
                after(c)
                c = mark(V.tensor_reduce(row_f[:, :], pick[:, :, :], AX.X, ALU.add))
                after(c)
                V.tensor_copy(row_i[:, par, t, :], row_f[:, :]).then_inc(row_ready, 1)

            def weigh(H, par):
                dve.wait_ge(wexp_ready, NT * (H + 1))
                c = mark(V.reciprocal(wrec[:, :], wsum[:, par, :]))
                after(c)
                V.tensor_tensor(wgt[:, par, :, :], wexp[:, par, :, :],
                                wrec[:, :].unsqueeze(2).to_broadcast([P, NT, TOPK]), ALU.mult)\
                    .then_inc(wgt_ready, 1)

            def attend(H, par):
                def row_max(it):
                    dve.wait_ge(s_ready, NT * H + it + 1)
                    V.tensor_reduce(nrow[:, it:it + 1], s_ps[it % 2][:, 0:(it + 1) * P], AX.X, ALU.max,
                                    negate=True).then_inc(max_ready, 1)

                row_max(0)
                row_max(1)
                for it in range(NT):
                    dve.wait_ge(pT_ready, NT * H + it + 1)
                    V.tensor_copy(probT[:, 0:it + 1, it * P:(it + 1) * P],
                                  pT_ps[:, 0:(it + 1) * P].rearrange("p (a b) -> p a b", b=P))\
                        .then_inc(pT_copied, 1)
                    if it + 2 < NT:
                        row_max(it + 2)
                c = mark(V.reciprocal(prec[:, :], psum_row[:, :]))
                after(c)
                dve.wait_ge(y_ready, H + 1)
                dve.wait_ge(y_used, H + 1)
                for it in range(NT):
                    last = V.scalar_tensor_tensor(yb[:, it, :], qoy_ps[:, it * P:(it + 1) * P], prec[:, it:it + 1],
                                                  yb[:, it, :], ALU.mult, ALU.add)
                last.then_inc(y_used, 1)

            for step in range(STEPS):
                early(0, step)
                late(0, step)
            for t in range(NT):
                find(0, 0, 0, t)
            weigh(0, 0)
            rewind()

            def batch(b, last):
                for h in range(NH):
                    H = NH * b + h
                    more = not (last and h == NH - 1)
                    for t in range(NT):
                        step = None if last else step_of(h, t)
                        if h == 0 and t == FIRST_UNIT - 1:
                            move_stream(b)
                        if step is not None:
                            early(b + 1, step)
                        if more:
                            find(H + 1, (h + 1) % NH, (h + 1) % 2, t)
                        if step is not None:
                            late(b + 1, step)
                    if more:
                        weigh(H + 1, (h + 1) % 2)
                    if h == 0:
                        dve.wait_ge(xb_moved, b + 1)
                    attend(H, h % 2)
                rewind()

            with dve.Fori(0, B - 1) as b:
                batch(b, False)
            batch(B - 1, True)


def kernel(x, adj, L0_gnn_W, L0_gnn_a, L0_ffn_Wg, L0_ffn_bg, L0_ffn_W1, L0_ffn_b1, L0_ffn_W2,
           L0_ffn_b2, L1_gnn_W, L1_gnn_a, L1_ffn_Wq_pk, L1_ffn_pk_keys, L1_ffn_Wq,
           L1_ffn_keys_table, L1_ffn_values_table, L1_ffn_Wo):
    import concourse.bacc as bacc
    from concourse.bass_utils import run_bass_kernel_spmd

    def lay(a):
        return np.ascontiguousarray(a)

    a = {k: np.asarray(v) for k, v in dict(
        x=x, adj=adj, w0=L0_gnn_W, a0=L0_gnn_a, wg=L0_ffn_Wg, bg=L0_ffn_bg, w1=L0_ffn_W1, b1=L0_ffn_b1,
        w2=L0_ffn_W2, b2=L0_ffn_b2, wl=L1_gnn_W, al=L1_gnn_a, wpk=L1_ffn_Wq_pk, keys=L1_ffn_pk_keys,
        wq=L1_ffn_Wq, kt=L1_ffn_keys_table, vt=L1_ffn_values_table, wo=L1_ffn_Wo).items()}
    arrays = {
        "x_in": lay(a["x"].reshape(B * N, D)),
        "adjT": lay(a["adj"].transpose(0, 2, 1).reshape(B * N, N)),
        "wgT0": lay(a["w0"].T), "wgT1": lay(a["wl"].T),
        "wg0": lay(a["w0"]), "wg1": lay(a["wl"]),
        "ac0": lay(a["a0"].reshape(2, D).T), "ac1": lay(a["al"].reshape(2, D).T),
        "gate_w": lay(a["wg"]), "gate_b": lay(a["bg"].reshape(1, E)),
        "w1": lay(a["w1"].transpose(1, 0, 2)),
        "b1": lay(a["b1"].reshape(E, HC, P).transpose(2, 0, 1)),
        "w2": lay(a["w2"].reshape(E, HC, P, D).transpose(2, 0, 1, 3)),
        "b2": lay(a["b2"].reshape(1, E * D)),
        "wpkT": lay(a["wpk"].reshape(D, 2, NH, DK).transpose(3, 2, 1, 0).reshape(DK, NH * 2 * D)),
        "keysT": lay(a["keys"].transpose(3, 2, 0, 1).reshape(DK, NH * 2 * NKEY)),
        "wq": lay(a["wq"]),
        "table": np.concatenate([a["kt"], a["vt"]], axis=1),
        "wo": lay(a["wo"].reshape(NH, D, D).transpose(1, 0, 2).reshape(D, NH * D)),
    }
    nc = bacc.Bacc("TRN2", target_bir_lowering=False, num_devices=1)
    args = [nc.dram_tensor(k, v.shape, mybir.dt.from_np(v.dtype), kind="ExternalInput").ap()
            for k, v in arrays.items()]
    args.append(nc.dram_tensor("out", (B * N, D), F32, kind="ExternalOutput").ap())
    program(nc, *args)
    r = run_bass_kernel_spmd(nc, [arrays], core_ids=[0])
    return np.asarray(r.results[0]["out"]).reshape(B, N, D)
```

```python
from contextlib import ExitStack

import numpy as np

import concourse.bass as bass
from concourse import mybir

F32 = mybir.dt.float32
I32 = mybir.dt.int32
U32 = mybir.dt.uint32
ALU = mybir.AluOpType
ACT = mybir.ActivationFunctionType
AX = mybir.AxisListType
ds = bass.ds

P = 128
B, N, D = 16, 512, 128
NT = N // P
E, HID = 8, 256
HC = HID // P
NH, DK, NKEY = 8, 64, 128
TOPK = 16
NKV = NKEY * NKEY
RECTS = [(0, 1, 16), (1, 1, 8), (2, 2, 5), (4, 4, 3), (8, 8, 1)]
NC = sum(na * nb for _, na, nb in RECTS)
EPS = 1e-5
SLOPE = 0.2
NEG_BIG = -9000000000000000.0
CAUSAL_NEG = -1e30
LOWEST = -3.0e38
GROUP = 8
GROUPS = TOPK // GROUP
RING = NT * GROUPS
HEADS = B * NH
HX = D + 2


def program(nc, x, adjT, wgT0, wgT1, wg0, wg1, ac0, ac1, gate_w, gate_b, w1, b1, w2, b2,
            wpkT, keysT, wq, table, wo, out):
    ctx = ExitStack()
    with ctx:
        def sb(name, shape, dt=F32):
            return ctx.enter_context(nc.sbuf_tensor(name, shape, dt))

        def sem(name):
            return ctx.enter_context(nc.semaphore(name))

        ident = sb("ident", [P, P])
        causal = sb("causal", [P, P])
        iota_i = sb("iota_i", [P, NC], I32)
        iota = sb("iota", [P, NC])
        head_row_i = sb("head_row_i", [P, NH], I32)
        head_row = sb("head_row", [P, NH])
        ones = sb("ones", [1, P])
        b2_sb = sb("b2_sb", [1, E * D])
        gb_sb = sb("gb_sb", [1, E])
        gw_sb = sb("gw_sb", [P, E])
        b1_sb = sb("b1_sb", [P, E, HC])
        w1_sb = sb("w1_sb", [P, E, HID])
        w2_sb = sb("w2_sb", [P, E, HC, D])
        ac_sb = sb("ac_sb", [P, 2, 2])
        wx = sb("wx", [P, 2, HX])
        wsrc = sb("wsrc", [P, 2, P])
        pk_w = sb("pk_w", [P, NH * 2 * NKEY])
        wq_sb = sb("wq_sb", [P, NH * D])
        wo_sb = sb("wo_sb", [P, NH * D])

        xb = sb("xb", [P, NT, D])
        adj_sb = sb("adj_sb", [P, NT, N], I32)
        neg = sb("neg", [P, NT, N])
        att = sb("att", [P, NT, N])
        xn = sb("xn", [P, NT, D])
        xT = sb("xT", [P, N])
        hx = sb("hx", [P, NT, HX])
        hid = sb("hid", [P, 4, N])
        ex = sb("ex", [P, NT, D])
        stats = sb("stats", [P, NT, 6])
        mv = sb("mv", [P, NT, 2])
        var_e = sb("var_e", [P, NT])
        std = sb("std", [P, NT])
        rstd = sb("rstd", [P, NT])
        colmax = sb("colmax", [P, NT])
        ncolmax = sb("ncolmax", [P, NT])
        colsum = sb("colsum", [P, NT])
        rcol = sb("rcol", [P, NT])
        rowsum = sb("rowsum", [P, NT])
        logits = sb("logits", [P, NT, E])
        top8 = sb("top8", [P, NT, 8])
        top8_i = sb("top8_i", [P, NT, 8], U32)
        top8_f = sb("top8_f", [P, NT, 8])
        gate = sb("gate", [P, NT, E])
        mark_cell = sb("mark_cell", [P, 1])

        xs = sb("xs", [P, N])
        qT = sb("qT", [P, 2, N])
        kv = sb("kv", [P, 2, NT, 2 * D])
        kT = sb("kT", [P, N])
        rows = sb("rows", [P, RING * GROUP, 2 * D])
        diag = sb("diag", [P, 2, TOPK, P])
        prob = sb("prob", [P, 2, N])
        probT = sb("probT", [P, NT, N])
        oT = sb("oT", [P, N])
        yb = sb("yb", [P, NT, D])
        half = sb("half", [P, 2, 2, TOPK])
        half_i = sb("half_i", [P, 2, TOPK], U32)
        rest = sb("rest", [P, 2, NKEY])
        cand = sb("cand", [P, 2, NC])
        cand2 = sb("cand2", [P, NC])
        best = sb("best", [P, 2, NT, TOPK])
        nbest = sb("nbest", [P, 2, NT])
        pos_i = sb("pos_i", [P, TOPK], U32)
        pos = sb("pos", [P, TOPK])
        pick = sb("pick", [P, TOPK, NC])
        row_f = sb("row_f", [P, TOPK])
        row_i = sb("row_i", [P, 2, NT, TOPK], U32)
        wexp = sb("wexp", [P, 2, NT, TOPK])
        wsum = sb("wsum", [P, 2, NT])
        wrec = sb("wrec", [P, NT])
        wgt = sb("wgt", [P, 2, NT, TOPK])
        nrow = sb("nrow", [P, NT])
        psum_row = sb("psum_row", [P, NT])
        prec = sb("prec", [P, NT])

        wpkT_sb = rows[0:DK, 0:8, :].rearrange("p a b -> p (a b)")
        keysT_sb = rows[0:DK, 8:16, :].rearrange("p a b -> p (a b)")
        wgT_sb = [rows[:, 16 + g, 0:D] for g in range(2)]

        bank = [ctx.enter_context(nc.psum_tensor(f"bank{i}", [P, 512], F32)) for i in range(8)]
        sim_ps = bank[0]
        hx_ps = msg_ps = up_ps = [bank[1], bank[2]]
        gate_ps = bank[1]
        kv_ps = bank[3]
        s_ps = down_ps = [bank[4], bank[5]]
        src_ps = bank[4]
        pT_ps = kT_ps = tr_ps = bank[6]
        qoy_ps = bank[7]

        PK_BANKS = (0, 3, 5, 7)

        turn_pool, turn_dve, turn_sp = sem("turn_pool"), sem("turn_dve"), sem("turn_sp")
        graph_weights_in, weights_in = sem("graph_weights_in"), sem("weights_in")
        made = sem("made")
        setup_mm, setup_cp = sem("setup_mm"), sem("setup_cp")
        chain = sem("chain")
        x_in, adj_in = sem("x_in"), sem("adj_in")
        var_ready, std_ready, xn_ready = sem("var_ready"), sem("std_ready"), sem("xn_ready")
        tr_ready, xT_ready = sem("tr_ready"), sem("xT_ready")
        src_ready, hx_ready, hx_copied = sem("src_ready"), sem("hx_ready"), sem("hx_copied")
        z_ready, masked, att_ready = sem("z_ready"), sem("masked"), sem("att_ready")
        rhs_ready, msg_ready = sem("rhs_ready"), sem("msg_ready")
        elu_in, elu_exp = sem("elu_in"), sem("elu_exp")
        gate_ready, gate_copied = sem("gate_ready"), sem("gate_copied")
        up_ready, gelu_done = sem("up_ready"), sem("gelu_done")
        down_ready, down_used = sem("down_ready"), sem("down_used")
        adj_used, xb_moved = sem("adj_used"), sem("xb_moved")
        y_out = sem("y_out")
        q_in, q_ready, q_copied = sem("q_in"), sem("q_ready"), sem("q_copied")
        sim_ready, sim_used = sem("sim_ready"), sem("sim_used")
        best_ready, wexp_ready, wgt_ready = sem("best_ready"), sem("wexp_ready"), sem("wgt_ready")
        row_ready = sem("row_ready")
        row_in = [sem(f"row_in{i}") for i in range(RING)]
        diag_ready, kv_group, kv_copied = sem("diag_ready"), sem("kv_group"), sem("kv_copied")
        kT_ready, kT_copied = sem("kT_ready"), sem("kT_copied")
        s_ready, max_ready, p_ready = sem("s_ready"), sem("max_ready"), sem("p_ready")
        pT_ready, pT_copied = sem("pT_ready"), sem("pT_copied")
        o_ready, o_copied, y_ready, y_used = sem("o_ready"), sem("o_copied"), sem("y_ready"), sem("y_used")


        x_v = x.rearrange("(n p) d -> p n d", p=P)
        adj_v = adjT.rearrange("(n p) i -> p n i", p=P)
        out_v = out.rearrange("(n p) d -> p n d", p=P)

        graph_loads = [
            (wgT_sb[0], wgT0), (wgT_sb[1], wgT1), (ac_sb[:, 0, :], ac0), (ac_sb[:, 1, :], ac1),
            (wx[:, 0, 0:D], wg0), (wx[:, 1, 0:D], wg1),
        ]
        weight_loads = [
            (wpkT_sb, wpkT), (keysT_sb, keysT), (gw_sb[:, :], gate_w), (gb_sb[:, :], gate_b),
            (b1_sb[:, :, :], b1), (b2_sb[:, :], b2), (w1_sb[:, :, :], w1), (w2_sb[:, :, :, :], w2),
            (wq_sb[:, :], wq), (wo_sb[:, :], wo),
        ]
        GRAPH_WEIGHTS, WEIGHTS = 16 * len(graph_loads), 16 * len(weight_loads)

        block = ctx.enter_context(nc.Block())

        NORM0, GRAPH0, NORM1, GATE, UP, NORM2, GRAPH1, NORM3 = 0, 1, 4, 5, 6, 15, 16, 19
        STEPS = 20
        MOVE_UNIT = (0, 1)
        TILES_WITH_STEP = [(2, 3), (0, 1, 2, 3), (1, 3), (1, 2, 3), (1, 3), (1, 2, 3), (0, 1, 2, 3), ()]
        UNITS_WITH_STEP = [(h, t) for h in range(NH) for t in TILES_WITH_STEP[h]]
        assert len(UNITS_WITH_STEP) == STEPS and MOVE_UNIT < UNITS_WITH_STEP[0]

        def step_of(h, t):
            return UNITS_WITH_STEP.index((h, t)) if (h, t) in UNITS_WITH_STEP else None

        @block.sync
        def _(sp):
            sp.sem_inc(y_out, 1)
            sp.dma_start(xb[:, :, :], x_v[:, 0:NT, :]).then_inc(x_in, 16)
            for dst, src in graph_loads:
                sp.dma_start(dst, src).then_inc(graph_weights_in, 16)
            sp.dma_start(adj_sb[:, :, :], adj_v[:, 0:NT, :]).then_inc(adj_in, 16)
            for dst, src in weight_loads:
                sp.dma_start(dst, src).then_inc(weights_in, 16)

            def load_front(f):
                sp.wait_ge(adj_used, f)
                sp.sem_inc(turn_sp, 1)
                sp.dma_start(adj_sb[:, :, :], adj_v[:, ds(NT * f, NT), :]).then_inc(adj_in, 16)
                sp.wait_ge(xb_moved, f)
                sp.sem_inc(turn_sp, 1)
                sp.dma_start(xb[:, :, :], x_v[:, ds(NT * f, NT), :]).then_inc(x_in, 16)

            def store_y(b):
                sp.wait_ge(y_used, NH * (b + 1) + 1)
                sp.sem_inc(turn_sp, 1)
                sp.dma_start(out_v[:, ds(NT * b, NT), :], yb[:, :, :]).then_inc(y_out, 16)
                sp.wait_ge(y_out, 16 * (b + 1) + 1)
                sp.sem_inc(turn_sp, 1)

            with sp.Fori(0, B - 1) as b:
                load_front(b + 1)
                store_y(b)
            for t in range(NT):
                sp.wait_ge(y_used, B * NH + t + 1)
                sp.dma_start(out_v[:, NT * (B - 1) + t, :], yb[:, t, :]).then_inc(y_out, 16)
            sp.wait_ge(y_out, 16 * (B - 1 + NT) + 1)

        @block.gpsimd
        def _(pool):
            pool.memset(ident[:, :], 0.0).then_inc(made, 1)
            pool.memset(causal[:, :], 0.0).then_inc(made, 1)
            pool.wait_ge(made, 2)
            pool.affine_select(out=ident[:, :], in_=ident[:, :], compare_op=ALU.not_equal, fill=1.0,
                               base=0, pattern=[[-1, P]], channel_multiplier=1).then_inc(made, 1)
            pool.affine_select(out=causal[:, :], in_=causal[:, :], compare_op=ALU.is_ge, fill=CAUSAL_NEG,
                               base=0, pattern=[[-1, P]], channel_multiplier=1).then_inc(made, 1)
            pool.iota(iota_i[:, :], [[1, NC]], base=0, channel_multiplier=0).then_inc(made, 1)
            pool.iota(head_row_i[:, :], [[NKV, NH]], base=0, channel_multiplier=0).then_inc(made, 1)
            pool.wait_ge(made, 6)

            with pool.Fori(0, HEADS // 2) as i:
                for par in range(2):
                    H = 2 * i + par
                    for t in range(NT):
                        pool.wait_ge(row_ready, NT * H + t + 1)
                        for g in range(GROUPS):
                            ring = GROUPS * t + g
                            pool.wait_ge(kv_group, GROUPS * (NT * H + t) + g + 1)
                            pool.sem_inc(turn_pool, 1)
                            for k in range(GROUP):
                                pool.indirect_dma_start(
                                    rows[:, GROUP * ring + k, :], None, table,
                                    bass.IndirectOffsetOnAxis(
                                        ap=row_i[:, par, t, GROUP * g + k:GROUP * g + k + 1], axis=0),
                                ).then_inc(row_in[ring], 16)

        @block.tensor
        def _(pe):
            mm = nc.tensor.matmul
            pe.wait_ge(graph_weights_in, GRAPH_WEIGHTS)
            for g in range(2):
                last = mm(bank[7][:, 2 * g:2 * g + 2], wgT_sb[g], ac_sb[:, g, :], start=True, stop=True)
            last.then_inc(setup_mm, 1)
            pe.sem_inc(tr_ready, 1)
            pe.wait_ge(setup_cp, 1)
            pe.wait_ge(made, 6)

            def query_keys():
                pe.wait_ge(weights_in, WEIGHTS)
                for c in range(NH * 2):
                    last = mm(bank[PK_BANKS[c // 4]][:, (c % 4) * P:(c % 4 + 1) * P],
                              wpkT_sb[:, c * P:(c + 1) * P], keysT_sb[:, c * P:(c + 1) * P],
                              start=True, stop=True)
                last.then_inc(setup_mm, 1)
                pe.sem_inc(kv_group, RING)

            def transposed(n):
                pe.wait_ge(xn_ready, n + 1)
                for t in range(NT):
                    last = nc.tensor.transpose(tr_ps[:, t * P:(t + 1) * P], xn[:, t, :], ident[:, :])
                last.then_inc(tr_ready, 1)

            def project(f, g):
                pe.wait_ge(xT_ready, 4 * f + 2 * g + 2)
                mm(src_ps[:, :], wsrc[:, g, :], xT[:, :], start=True, stop=True).then_inc(src_ready, 1)
                for t in range(NT):
                    last = mm(hx_ps[t // 2][:, (t % 2) * HX:(t % 2 + 1) * HX], xT[:, t * P:(t + 1) * P],
                              wx[:, g, :], start=True, stop=True)
                last.then_inc(hx_ready, 1)

            def messages(f, g):
                width = D + g
                pe.wait_ge(rhs_ready, 2 * f + g + 1)
                pe.wait_ge(att_ready, NT * (2 * f + g + 1))
                for it in range(NT):
                    for jt in range(NT):
                        last = mm(msg_ps[it // 2][:, (it % 2) * HX:(it % 2) * HX + width],
                                  att[:, jt, it * P:(it + 1) * P], hx[:, jt, 0:width],
                                  start=(jt == 0), stop=(jt == NT - 1))
                last.then_inc(msg_ready, 1)

            def gates(f):
                pe.wait_ge(xT_ready, 4 * f + 3)
                for t in range(NT):
                    o = gate_ps[:, t * E:(t + 1) * E]
                    mm(o, xT[:, t * P:(t + 1) * P], gw_sb[:, :], start=True, stop=False)
                    last = mm(o, ones[:, :], gb_sb[:, :], start=False, stop=True)
                last.then_inc(gate_ready, 1)

            def up(f, e):
                if e == 0:
                    pe.wait_ge(gate_copied, f + 1)
                for c in range(HC):
                    if e:
                        pe.wait_ge(gelu_done, HC * (E * f + e - 1) + c + 1)
                    mm(up_ps[c][:, :], w1_sb[:, e, c * P:(c + 1) * P], xT[:, :],
                       start=True, stop=True).then_inc(up_ready, 1)

            def down(f, e):
                pe.wait_ge(gelu_done, HC * (E * f + e + 1))
                if e >= 2:
                    pe.wait_ge(down_used, E * f + e - 1)
                for t in range(NT):
                    o = down_ps[e % 2][:, t * P:(t + 1) * P]
                    for c in range(HC):
                        mm(o, hid[:, (HC * e + c) % 4, t * P:(t + 1) * P], w2_sb[:, e, c, :],
                           start=(c == 0), stop=False)
                    last = mm(o, ones[:, :], b2_sb[:, e * D:(e + 1) * D], start=False, stop=True)
                last.then_inc(down_ready, 1)

            def early(f, step):
                if step in (GRAPH0, GRAPH1):
                    project(f, int(step == GRAPH1))
                if step == GATE:
                    gates(f)
                if UP <= step < UP + E:
                    up(f, step - UP)
                if UP + 1 <= step <= UP + E:
                    down(f, step - UP - 1)

            def late(f, step, attention_next):
                if step in (NORM0, NORM1, NORM2, NORM3):
                    n = 4 * f + (NORM0, NORM1, NORM2, NORM3).index(step)
                    transposed(n)
                    if attention_next:
                        pe.wait_ge(xT_ready, n + 2)
                if step in (GRAPH0, GRAPH1) and attention_next:
                    pe.wait_ge(z_ready, NT * (2 * f + int(step == GRAPH1) + 1))
                if step in (GRAPH0 + 1, GRAPH1 + 1):
                    messages(f, int(step == GRAPH1 + 1))
                if UP + 1 <= step <= UP + E and attention_next:
                    pe.wait_ge(down_used, E * f + step - UP)

            def query(H, h, first=False):
                pe.wait_ge(q_in, H // NH + 1 if first else (H + NH - h) // NH)
                if not first:
                    pe.wait_ge(y_used, H)
                mm(qoy_ps[:, :], wq_sb[:, h * D:(h + 1) * D], xs[:, :], start=True, stop=True)\
                    .then_inc(q_ready, 1)

            def scores(H, h, t, first=False):
                if not first:
                    pe.wait_ge(sim_used, NT * H + t)
                elif t:
                    pe.wait_ge(sim_used, t)
                else:
                    pe.wait_ge(xT_ready, 5)
                mm(sim_ps[:, 0:2 * NKEY], (xT if first else xs)[:, t * P:(t + 1) * P],
                   pk_w[:, h * 2 * NKEY:(h + 1) * 2 * NKEY], start=True, stop=True).then_inc(sim_ready, 1)

            def combine(H, par, t):
                n = NT * H + t
                pe.wait_ge(kv_copied, n + 1)
                for k in range(TOPK):
                    slot = TOPK * t + k
                    if k % GROUP == 0:
                        pe.wait_ge(diag_ready, GROUPS * n + k // GROUP + 1)
                        pe.wait_ge(row_in[slot // GROUP], 16 * GROUP * (H + 1))
                    last = mm(kv_ps[:, 0:2 * D], diag[:, t % 2, k, :], rows[:, slot, :],
                              start=(k == 0), stop=(k == TOPK - 1))
                    if k % GROUP == GROUP - 1:
                        last.then_inc(kv_group, 1)

            def transpose_k(par, it):
                return nc.tensor.transpose(kT_ps[:, it * P:(it + 1) * P], kv[:, par, it, 0:D], ident[:, :])

            def s_tile(H, par, it):
                if it >= 2:
                    pe.wait_ge(p_ready, NT * H + it - 1)
                q = qT[:, par, it * P:(it + 1) * P]
                mm(s_ps[it % 2][:, 0:(it + 1) * P], q, kT[:, 0:(it + 1) * P], start=True, stop=False,
                   skip_group_check=True)
                mm(s_ps[it % 2][:, it * P:(it + 1) * P], ident[:, :], causal[:, :], start=False, stop=True,
                   skip_group_check=True).then_inc(s_ready, 1)

            def t_tile(H, it):
                pe.wait_ge(p_ready, NT * H + it + 1)
                if it:
                    pe.wait_ge(pT_copied, NT * H + it)
                for jt in range(it + 1):
                    last = nc.tensor.transpose(pT_ps[:, jt * P:(jt + 1) * P],
                                               prob[:, it % 2, jt * P:(jt + 1) * P], ident[:, :])
                last.then_inc(pT_ready, 1)

            def o_tile(par, it):
                for jt in range(it + 1):
                    last = mm(qoy_ps[:, it * P:(it + 1) * P], kv[:, par, jt, D:2 * D],
                              probT[:, jt, it * P:(it + 1) * P], start=(jt == 0), stop=(jt == it))
                return last

            def y_tile(h, it):
                return mm(qoy_ps[:, it * P:(it + 1) * P], oT[:, it * P:(it + 1) * P],
                          wo_sb[:, h * D:(h + 1) * D], start=True, stop=True)

            def attend(H, h, par):
                pe.wait_ge(kv_copied, NT * (H + 1) + 1)
                for it in range(NT):
                    last = transpose_k(par, it)
                last.then_inc(kT_ready, 1)
                pe.wait_ge(kT_copied, H + 1)
                s_tile(H, par, 0)
                s_tile(H, par, 1)
                for it in range(NT):
                    t_tile(H, it)
                    if it + 2 < NT:
                        s_tile(H, par, it + 2)
                pe.wait_ge(q_copied, H + 2)
                pe.wait_ge(pT_copied, NT * (H + 1))
                for jt in range(NT):
                    last = mm(qoy_ps[:, jt * P:N], kv[:, par, jt, D:2 * D], probT[:, jt, jt * P:N],
                              start=(jt == 0), stop=(jt == NT - 1), skip_group_check=True)
                last.then_inc(o_ready, 1)
                pe.wait_ge(o_copied, H + 1)
                for it in range(NT):
                    last = y_tile(h, it)
                last.then_inc(y_ready, 1)

            def attend_tile(H, h, par, it):
                pe.wait_ge(kv_copied, NT * H + it + 2)
                transpose_k(par, it).then_inc(kT_ready, 1)
                pe.wait_ge(kT_copied, H + it + 1)
                s_tile(H, par, it)
                t_tile(H, it)
                pe.wait_ge(y_used, H + it + 1)
                pe.wait_ge(pT_copied, NT * H + it + 1)
                o_tile(par, it).then_inc(o_ready, 1)
                pe.wait_ge(o_copied, H + it + 1)
                y_tile(h, it).then_inc(y_ready, 1)

            for step in range(STEPS):
                early(0, step)
                if step == GATE:
                    pe.wait_ge(setup_cp, 2)
                late(0, step, False)
                if step == GRAPH0 + 1:
                    query_keys()
            for t in range(NT):
                scores(0, 0, t, first=True)
                if t == 0:
                    query(0, 0, first=True)
            pe.wait_ge(q_copied, 1)

            def batch(b, last):
                for h in range(NH):
                    H = NH * b + h
                    more = not (last and h == NH - 1)
                    if more:
                        query(H + 1, (h + 1) % NH)
                    for t in range(NT):
                        step = None if last else step_of(h, t)
                        if step is not None:
                            early(b + 1, step)
                        if more:
                            scores(H + 1, (h + 1) % NH, t)
                        combine(H, h % 2, t)
                        if step is not None:
                            late(b + 1, step, t == NT - 1 or step == UP + E)
                        if not more:
                            attend_tile(H, h, h % 2, t)
                    if more:
                        attend(H, h, h % 2)

            with pe.Fori(0, B - 1) as b:
                batch(b, False)
            batch(B - 1, True)

        @block.scalar
        def _(act):
            A = nc.scalar.activation
            act.sem_inc(kv_copied, 1)
            act.sem_inc(xT_ready, 1)

            def std_dev(n):
                act.wait_ge(var_ready, n + 1)
                A(std[:, :], var_e[:, :], ACT.Sqrt).then_inc(std_ready, 1)

            def copy_xT(n):
                act.wait_ge(tr_ready, n + 2)
                A(xT[:, :], tr_ps[:, :], ACT.Copy).then_inc(xT_ready, 1)

            def pair_scores(f, g):
                act.wait_ge(hx_ready, 2 * f + g + 1)
                for q in range(2):
                    last = A(hx[:, 2 * q:2 * q + 2, :].rearrange("p a b -> p (a b)"),
                             hx_ps[q][:, 0:2 * HX], ACT.Copy)
                last.then_inc(hx_copied, 1)
                act.wait_ge(hx_copied, 2 * f + g + 1)
                for t in range(NT):
                    A(att[:, t, :], src_ps[:, :], ACT.Identity, bias=hx[:, t, D + 1:D + 2])\
                        .then_inc(z_ready, 1)

            def pair_weights(f, g):
                for t in range(NT):
                    act.wait_ge(masked, NT * (2 * f + g) + t + 1)
                    if g == 0:
                        A(att[:, t, :], att[:, t, :], ACT.Exp, bias=ncolmax[:, t:t + 1],
                          accum_out=colsum[:, t:t + 1]).then_inc(att_ready, 1)
                    else:
                        A(att[:, t, :], att[:, t, :], ACT.Exp, scale=-1.0).then_inc(att_ready, 1)

            def elu(f, g):
                act.wait_ge(elu_in, 2 * f + g + 1)
                A(ex[:, :, :], ex[:, :, :], ACT.Exp).then_inc(elu_exp, 1)

            def gelu(f, e):
                for c in range(HC):
                    u = HC * e + c
                    act.wait_ge(up_ready, HC * E * f + u + 1)
                    if e >= 2:
                        act.wait_ge(down_ready, E * f + e - 1)
                    A(hid[:, u % 4, :], up_ps[c][:, :], ACT.Gelu, bias=b1_sb[:, e, c:c + 1])\
                        .then_inc(gelu_done, 1)

            def early(f, step):
                if step in (NORM0, NORM1, NORM2, NORM3):
                    std_dev(4 * f + (NORM0, NORM1, NORM2, NORM3).index(step))
                if step in (GRAPH0, GRAPH1):
                    pair_scores(f, int(step == GRAPH1))
                if UP <= step < UP + E:
                    gelu(f, step - UP)
                if step in (GRAPH0 + 1, GRAPH1 + 1):
                    pair_weights(f, int(step == GRAPH1 + 1))

            def late(f, step):
                if step in (NORM0, NORM1, NORM2, NORM3):
                    copy_xT(4 * f + (NORM0, NORM1, NORM2, NORM3).index(step))
                if step in (GRAPH0 + 2, GRAPH1 + 2):
                    elu(f, int(step == GRAPH1 + 2))

            def next_batch(f):
                act.wait_ge(xT_ready, 4 * f + 5)
                A(xs[:, :], xT[:, :], ACT.Copy).then_inc(q_in, 1)

            def query(H, par):
                act.wait_ge(q_ready, H + 1)
                A(qT[:, par, :], qoy_ps[:, :], ACT.Copy, scale=float(D) ** -0.5).then_inc(q_copied, 1)

            def best_exp(H, par, t):
                act.wait_ge(best_ready, NT * H + t + 1)
                A(wexp[:, par, t, :], best[:, par, t, :], ACT.Exp, bias=nbest[:, par, t:t + 1],
                  accum_out=wsum[:, par, t:t + 1]).then_inc(wexp_ready, 1)

            def diagonals(H, par, t):
                if t == 0:
                    act.wait_ge(wgt_ready, H + 1)
                for k in range(TOPK):
                    last = A(diag[:, t % 2, k, :], ident[:, :], ACT.Copy, scale=wgt[:, par, t, k:k + 1])
                    if k % GROUP == GROUP - 1:
                        last.then_inc(diag_ready, 1)

            def copy_kv(H, par, t):
                act.wait_ge(kv_group, GROUPS * (NT * H + t + 1) + RING)
                A(kv[:, par, t, :], kv_ps[:, 0:2 * D], ACT.Copy).then_inc(kv_copied, 1)

            def row_exp(H, it):
                act.wait_ge(max_ready, NT * H + it + 1)
                if it >= 2:
                    act.wait_ge(pT_ready, NT * H + it - 1)
                w = (it + 1) * P
                A(prob[:, it % 2, 0:w], s_ps[it % 2][:, 0:w], ACT.Exp, bias=nrow[:, it:it + 1],
                  accum_out=psum_row[:, it:it + 1]).then_inc(p_ready, 1)

            def attend_tile(H, it):
                row_exp(H, it)
                act.wait_ge(o_ready, H + it + 1)
                A(oT[:, it * P:(it + 1) * P], qoy_ps[:, it * P:(it + 1) * P], ACT.Copy).then_inc(o_copied, 1)

            def attend(H, par):
                for it in range(NT):
                    row_exp(H, it)
                diagonals(H + 1, 1 - par, 0)
                act.wait_ge(o_ready, H + 1)
                A(oT[:, :], qoy_ps[:, :], ACT.Copy).then_inc(o_copied, 1)

            for step in range(STEPS):
                if step == UP:
                    act.wait_ge(weights_in, WEIGHTS)
                early(0, step)
                late(0, step)
            next_batch(0)
            query(0, 0)
            for t in range(NT):
                best_exp(0, 0, t)
            diagonals(0, 0, 0)

            def batch(b, last):
                for h in range(NH):
                    H = NH * b + h
                    more = not (last and h == NH - 1)
                    if more:
                        if h == NH - 1:
                            next_batch(b + 1)
                        query(H + 1, (h + 1) % 2)
                    for t in range(NT):
                        step = None if last else step_of(h, t)
                        if step is not None:
                            early(b + 1, step)
                        if t + 1 < NT:
                            diagonals(H, h % 2, t + 1)
                        copy_kv(H, h % 2, t)
                        if more:
                            best_exp(H + 1, (h + 1) % 2, t)
                        if step is not None:
                            late(b + 1, step)
                        if not more:
                            attend_tile(H, t)
                    if more:
                        attend(H, h % 2)

            with act.Fori(0, B - 1) as b:
                batch(b, False)
            batch(B - 1, True)

        @block.vector
        def _(dve):
            V = nc.vector
            count = [0]

            def mark(ins):
                count[0] += 1
                ins.then_inc(chain, 1)
                return count[0]

            def after(value):
                dve.wait_ge(chain, value)

            def rewind():
                after(count[0])
                dve.sem_clear(chain)
                count[0] = 0

            dve.wait_ge(made, 6)
            V.tensor_copy(iota[:, :], iota_i[:, :])
            V.tensor_copy(head_row[:, :], head_row_i[:, :])
            V.memset(ones[:, :], 1.0)
            V.memset(mark_cell[:, :], 0.0).then_inc(y_used, 1)
            dve.wait_ge(y_used, 1)

            def graph_scores():
                dve.wait_ge(setup_mm, 1)
                for g in range(2):
                    V.tensor_copy(wx[:, g, D:D + 2], bank[7][:, 2 * g:2 * g + 2])
                    last = V.tensor_copy(wsrc[:, g, :], bank[7][:, 2 * g:2 * g + 1].to_broadcast([P, P]))
                last.then_inc(setup_cp, 1)

            def query_keys():
                dve.wait_ge(setup_mm, 2)
                for q in range(4):
                    last = V.tensor_copy(pk_w[:, q * 512:(q + 1) * 512], bank[PK_BANKS[q]][:, :])
                last.then_inc(setup_cp, 1)

            def statistics(f, n):
                if n == 0:
                    dve.wait_ge(x_in, 16 * (f + 1))
                    dve.sem_inc(turn_dve, 1)
                for t in range(NT):
                    c = mark(V.bn_stats(stats[:, t, :], xb[:, t, :]))
                after(c)
                for t in range(NT):
                    c = mark(V.bn_aggr(mv[:, t, :], stats[:, t, :]))
                after(c)
                V.tensor_scalar(var_e[:, :], mv[:, :, 1], EPS, None, ALU.add).then_inc(var_ready, 1)

            def normalise(f, n):
                dve.wait_ge(std_ready, 4 * f + n + 1)
                c = mark(V.reciprocal(rstd[:, :], std[:, :]))
                after(c)
                dve.wait_ge(tr_ready, 4 * f + n + 1)
                for t in range(NT):
                    last = V.tensor_scalar(xn[:, t, :], xb[:, t, :], mv[:, t, 0:1], rstd[:, t:t + 1],
                                           ALU.subtract, ALU.mult)
                last.then_inc(xn_ready, 1)

            def mask_pairs(f, g):
                if g == 0:
                    dve.wait_ge(adj_in, 16 * (f + 1))
                c = mark(V.tensor_scalar(neg[:, :, :], adj_sb[:, :, :], 0.0, -NEG_BIG if g else NEG_BIG,
                                         ALU.is_equal if g else ALU.is_le, ALU.mult))
                cs = []
                for t in range(NT):
                    dve.wait_ge(z_ready, NT * (2 * f + g) + t + 1)
                    cs.append(mark(V.scalar_tensor_tensor(att[:, t, :], att[:, t, :], SLOPE, att[:, t, :],
                                                          ALU.mult, ALU.max)))
                if g == 0:
                    for t in range(NT):
                        after(max(c, cs[t]))
                        cs[t] = mark(V.tensor_tensor_reduce(
                            out=att[:, t, :], in0=att[:, t, :], in1=neg[:, t, :], scale=1.0, scalar=LOWEST,
                            op0=ALU.add, op1=ALU.max, accum_out=colmax[:, t:t + 1]))
                    for t in range(NT):
                        after(cs[t])
                        V.tensor_scalar(ncolmax[:, t:t + 1], colmax[:, t:t + 1], -1.0, None, ALU.mult)\
                            .then_inc(masked, 1)
                else:
                    for t in range(NT):
                        after(max(c, cs[t]))
                        V.tensor_tensor(att[:, t, :], att[:, t, :], neg[:, t, :], ALU.add).then_inc(masked, 1)
                    V.memset(mark_cell[:, :], 0.0).then_inc(adj_used, 1)

            def right_side(f, g):
                if g == 0:
                    dve.wait_ge(att_ready, NT * (2 * f + 1))
                    c = mark(V.reciprocal(rcol[:, :], colsum[:, :]))
                    after(c)
                    dve.wait_ge(hx_copied, 2 * f + 1)
                    for t in range(NT):
                        last = V.tensor_scalar(hx[:, t, 0:D], hx[:, t, 0:D], rcol[:, t:t + 1], None, ALU.mult)
                    last.then_inc(rhs_ready, 1)
                else:
                    dve.wait_ge(hx_copied, 2 * f + 2)
                    V.memset(hx[:, :, D:D + 1], 1.0).then_inc(rhs_ready, 1)

            def received(f, g):
                dve.wait_ge(msg_ready, 2 * f + g + 1)
                msg = [msg_ps[q][:, 0:2 * HX].rearrange("p (a b) -> p a b", b=HX) for q in range(2)]
                if g == 0:
                    for q in range(2):
                        c = mark(V.tensor_copy(xn[:, 2 * q:2 * q + 2, :], msg[q][:, :, 0:D]))
                else:
                    for q in range(2):
                        c = mark(V.tensor_copy(rowsum[:, 2 * q:2 * q + 2], msg[q][:, :, D]))
                    after(c)
                    c = mark(V.scalar_tensor_tensor(rowsum[:, :], rowsum[:, :], 0.0, rowsum[:, :],
                                                    ALU.is_equal, ALU.add))
                    after(c)
                    c = mark(V.reciprocal(rcol[:, :], rowsum[:, :]))
                    after(c)
                    for t in range(NT):
                        c = mark(V.tensor_scalar(xn[:, t, :], msg[t // 2][:, t % 2, 0:D], rcol[:, t:t + 1],
                                                 None, ALU.mult))
                after(c)
                V.tensor_scalar(ex[:, :, :], xn[:, :, :], 0.0, None, ALU.min).then_inc(elu_in, 1)
                after(mark(V.scalar_tensor_tensor(xn[:, :, :], xn[:, :, :], 0.0, xb[:, :, :], ALU.max, ALU.add)))

            def elu(f, g):
                dve.wait_ge(elu_exp, 2 * f + g + 1)
                after(mark(V.scalar_tensor_tensor(xb[:, :, :], ex[:, :, :], -1.0, xn[:, :, :], ALU.add, ALU.add)))

            def choose(f):
                dve.wait_ge(gate_ready, f + 1)
                V.tensor_copy(logits[:, :, :], gate_ps[:, 0:NT * E].rearrange("p (a b) -> p a b", b=E))\
                    .then_inc(gate_copied, 1)
                dve.wait_ge(gate_copied, f + 1)
                dve.sem_inc(turn_dve, 1)
                for t in range(NT):
                    c = mark(V.max(top8[:, t, :], logits[:, t, :]))
                after(c)
                for t in range(NT):
                    c = mark(V.max_index(top8_i[:, t, :], top8[:, t, :], logits[:, t, :]))
                after(c)
                after(mark(V.tensor_copy(top8_f[:, :, 0:2], top8_i[:, :, 0:2])))
                for t in range(NT):
                    c = mark(V.tensor_scalar(gate[:, t, :], iota[:, 0:E], top8_f[:, t, 0:1], None, ALU.is_equal))
                after(c)
                for t in range(NT):
                    c = mark(V.scalar_tensor_tensor(gate[:, t, :], iota[:, 0:E], top8_f[:, t, 1:2], gate[:, t, :],
                                                    ALU.is_equal, ALU.add))
                after(c)

            def add_expert(f, e):
                dve.wait_ge(down_ready, E * f + e + 1)
                for t in range(NT):
                    c = mark(V.scalar_tensor_tensor(
                        xb[:, t, :], down_ps[e % 2][:, t * P:(t + 1) * P], gate[:, t, e:e + 1],
                        xb[:, t, :], ALU.mult, ALU.add))
                after(c)
                V.memset(mark_cell[:, :], 0.0).then_inc(down_used, 1)

            def early(f, step):
                if step in (NORM0, NORM1, NORM2, NORM3):
                    statistics(f, (NORM0, NORM1, NORM2, NORM3).index(step))
                if step in (GRAPH0 + 2, GRAPH1 + 2):
                    received(f, int(step == GRAPH1 + 2))

            def late(f, step):
                if step in (NORM0, NORM1, NORM2, NORM3):
                    normalise(f, (NORM0, NORM1, NORM2, NORM3).index(step))
                if step in (GRAPH0, GRAPH1):
                    mask_pairs(f, int(step == GRAPH1))
                if step in (GRAPH0 + 1, GRAPH1 + 1):
                    right_side(f, int(step == GRAPH1 + 1))
                if step in (GRAPH0 + 2, GRAPH1 + 2):
                    elu(f, int(step == GRAPH1 + 2))
                if step == GATE:
                    choose(f)
                if UP + 1 <= step <= UP + E:
                    add_expert(f, step - UP - 1)

            def move_stream(f):
                dve.wait_ge(y_out, 16 * f + 1)
                V.tensor_copy(yb[:, :, :], xb[:, :, :]).then_inc(xb_moved, 1)

            def find(H, h, par, t):
                n = NT * H + t
                sim = [sim_ps[:, p * NKEY:(p + 1) * NKEY] for p in range(2)]
                dve.wait_ge(sim_ready, n + 1)
                dve.sem_inc(turn_dve, 1)
                c = [mark(V.max(half[:, 0, p, 0:8], sim[p])) for p in range(2)]
                m = [0, 0]
                for p in range(2):
                    after(c[p])
                    m[p] = mark(V.match_replace(rest[:, p, :], half[:, 0, p, 0:8], sim[p], LOWEST))
                for p in range(2):
                    ins = V.max_index(half_i[:, p, 0:8], half[:, 0, p, 0:8], sim[p])
                    if p == 1:
                        ins.then_inc(sim_used, 1)
                    else:
                        mark(ins)
                for p in range(2):
                    after(m[p])
                    c[p] = mark(V.max(half[:, 0, p, 8:16], rest[:, p, :]))
                for p in range(2):
                    after(c[p])
                    c[p] = mark(V.max_index(half_i[:, p, 8:16], half[:, 0, p, 8:16], rest[:, p, :]))
                after(c[0])
                mark(V.tensor_scalar(half[:, 1, 0, :], half_i[:, 0, :], head_row[:, h:h + 1], None, ALU.add))
                after(c[1])
                c = mark(V.tensor_scalar(half[:, 1, 1, :], half_i[:, 1, :], float(NKEY), None, ALU.mult))
                after(c)
                o = 0
                for a, na, nb in RECTS:
                    shape = [P, 2, na, nb]
                    c = mark(V.tensor_tensor(
                        cand[:, :, o:o + na * nb].rearrange("p k (a b) -> p k a b", b=nb),
                        half[:, :, 0, a:a + na].unsqueeze(3).to_broadcast(shape),
                        half[:, :, 1, 0:nb].unsqueeze(2).to_broadcast(shape), ALU.add))
                    o += na * nb
                after(c)
                c = mark(V.max(best[:, par, t, 0:8], cand[:, 0, :]))
                after(c)
                c = mark(V.match_replace(cand2[:, :], best[:, par, t, 0:8], cand[:, 0, :], LOWEST))
                mark(V.max_index(pos_i[:, 0:8], best[:, par, t, 0:8], cand[:, 0, :]))
                mark(V.tensor_scalar(nbest[:, par, t:t + 1], best[:, par, t, 0:1], -1.0, None, ALU.mult))
                after(c)
                c = mark(V.max(best[:, par, t, 8:16], cand2[:, :]))
                after(c)
                c = mark(V.max_index(pos_i[:, 8:16], best[:, par, t, 8:16], cand2[:, :]))
                after(c)
                V.tensor_copy(pos[:, :], pos_i[:, :]).then_inc(best_ready, 1)
                dve.wait_ge(best_ready, n + 1)
                shape = [P, TOPK, NC]
                c = mark(V.tensor_tensor(pick[:, :, :], iota[:, :].unsqueeze(1).to_broadcast(shape),
                                         pos[:, :].unsqueeze(2).to_broadcast(shape), ALU.is_equal))
                after(c)
                c = mark(V.tensor_tensor(pick[:, :, :], pick[:, :, :],
                                         cand[:, 1, :].unsqueeze(1).to_broadcast(shape), ALU.mult))
                after(c)
                c = mark(V.tensor_reduce(row_f[:, :], pick[:, :, :], AX.X, ALU.add))
                after(c)
                V.tensor_copy(row_i[:, par, t, :], row_f[:, :]).then_inc(row_ready, 1)

            def weigh(H, par):
                dve.wait_ge(wexp_ready, NT * (H + 1))
                c = mark(V.reciprocal(wrec[:, :], wsum[:, par, :]))
                after(c)
                V.tensor_tensor(wgt[:, par, :, :], wexp[:, par, :, :],
                                wrec[:, :].unsqueeze(2).to_broadcast([P, NT, TOPK]), ALU.mult)\
                    .then_inc(wgt_ready, 1)

            def row_max(H, it):
                dve.wait_ge(s_ready, NT * H + it + 1)
                V.tensor_reduce(nrow[:, it:it + 1], s_ps[it % 2][:, 0:(it + 1) * P], AX.X, ALU.max,
                                negate=True).then_inc(max_ready, 1)

            def copy_pT(H, it):
                dve.wait_ge(pT_ready, NT * H + it + 1)
                V.tensor_copy(probT[:, 0:it + 1, it * P:(it + 1) * P],
                              pT_ps[:, 0:(it + 1) * P].rearrange("p (a b) -> p a b", b=P))\
                    .then_inc(pT_copied, 1)

            def copy_kT(value, first, n):
                dve.wait_ge(kT_ready, value)
                V.tensor_copy(kT[:, first * P:(first + n) * P], kT_ps[:, first * P:(first + n) * P])\
                    .then_inc(kT_copied, 1)

            def add_y(it):
                return V.scalar_tensor_tensor(yb[:, it, :], qoy_ps[:, it * P:(it + 1) * P], prec[:, it:it + 1],
                                              yb[:, it, :], ALU.mult, ALU.add)

            def attend(H):
                copy_kT(H + 1, 0, NT)
                row_max(H, 0)
                row_max(H, 1)
                for it in range(NT):
                    copy_pT(H, it)
                    if it + 2 < NT:
                        row_max(H, it + 2)
                c = mark(V.reciprocal(prec[:, :], psum_row[:, :]))
                after(c)
                dve.wait_ge(y_ready, H + 1)
                dve.wait_ge(y_used, H + 1)
                for it in range(NT):
                    last = add_y(it)
                last.then_inc(y_used, 1)

            def attend_tile(H, it):
                copy_kT(H + it + 1, it, 1)
                row_max(H, it)
                copy_pT(H, it)
                c = mark(V.reciprocal(prec[:, it:it + 1], psum_row[:, it:it + 1]))
                after(c)
                dve.wait_ge(y_ready, H + it + 1)
                dve.wait_ge(y_used, H + 1)
                add_y(it).then_inc(y_used, 1)

            for step in range(STEPS):
                early(0, step)
                if step == NORM0:
                    graph_scores()
                late(0, step)
                if step == NORM1:
                    query_keys()
            for t in range(NT):
                find(0, 0, 0, t)
            weigh(0, 0)
            rewind()

            def batch(b, last):
                for h in range(NH):
                    H = NH * b + h
                    more = not (last and h == NH - 1)
                    for t in range(NT):
                        step = None if last else step_of(h, t)
                        if (h, t) == MOVE_UNIT:
                            move_stream(b)
                        if step is not None:
                            early(b + 1, step)
                        if more:
                            find(H + 1, (h + 1) % NH, (h + 1) % 2, t)
                        if step is not None:
                            late(b + 1, step)
                        if not more:
                            attend_tile(H, t)
                    if more:
                        weigh(H + 1, (h + 1) % 2)
                        if h == 0:
                            dve.wait_ge(xb_moved, b + 1)
                        attend(H)
                rewind()

            with dve.Fori(0, B - 1) as b:
                batch(b, False)
            batch(B - 1, True)


def kernel(x, adj, L0_gnn_W, L0_gnn_a, L0_ffn_Wg, L0_ffn_bg, L0_ffn_W1, L0_ffn_b1, L0_ffn_W2,
           L0_ffn_b2, L1_gnn_W, L1_gnn_a, L1_ffn_Wq_pk, L1_ffn_pk_keys, L1_ffn_Wq,
           L1_ffn_keys_table, L1_ffn_values_table, L1_ffn_Wo):
    import concourse.bacc as bacc
    from concourse.bass_utils import run_bass_kernel_spmd

    def lay(a):
        return np.ascontiguousarray(a)

    a = {k: np.asarray(v) for k, v in dict(
        x=x, adj=adj, w0=L0_gnn_W, a0=L0_gnn_a, wg=L0_ffn_Wg, bg=L0_ffn_bg, w1=L0_ffn_W1, b1=L0_ffn_b1,
        w2=L0_ffn_W2, b2=L0_ffn_b2, wl=L1_gnn_W, al=L1_gnn_a, wpk=L1_ffn_Wq_pk, keys=L1_ffn_pk_keys,
        wq=L1_ffn_Wq, kt=L1_ffn_keys_table, vt=L1_ffn_values_table, wo=L1_ffn_Wo).items()}
    arrays = {
        "x_in": lay(a["x"].reshape(B * N, D)),
        "adjT": lay(a["adj"].transpose(0, 2, 1).reshape(B * N, N)),
        "wgT0": lay(a["w0"].T), "wgT1": lay(a["wl"].T),
        "wg0": lay(a["w0"]), "wg1": lay(a["wl"]),
        "ac0": lay(a["a0"].reshape(2, D).T), "ac1": lay(a["al"].reshape(2, D).T),
        "gate_w": lay(a["wg"]), "gate_b": lay(a["bg"].reshape(1, E)),
        "w1": lay(a["w1"].transpose(1, 0, 2)),
        "b1": lay(a["b1"].reshape(E, HC, P).transpose(2, 0, 1)),
        "w2": lay(a["w2"].reshape(E, HC, P, D).transpose(2, 0, 1, 3)),
        "b2": lay(a["b2"].reshape(1, E * D)),
        "wpkT": lay(a["wpk"].reshape(D, 2, NH, DK).transpose(3, 2, 1, 0).reshape(DK, NH * 2 * D)),
        "keysT": lay(a["keys"].transpose(3, 2, 0, 1).reshape(DK, NH * 2 * NKEY)),
        "wq": lay(a["wq"]),
        "table": np.concatenate([a["kt"], a["vt"]], axis=1),
        "wo": lay(a["wo"].reshape(NH, D, D).transpose(1, 0, 2).reshape(D, NH * D)),
    }
    nc = bacc.Bacc("TRN2", target_bir_lowering=False, num_devices=1)
    args = [nc.dram_tensor(k, v.shape, mybir.dt.from_np(v.dtype), kind="ExternalInput").ap()
            for k, v in arrays.items()]
    args.append(nc.dram_tensor("out", (B * N, D), F32, kind="ExternalOutput").ap())
    program(nc, *args)
    r = run_bass_kernel_spmd(nc, [arrays], core_ids=[0])
    return np.asarray(r.results[0]["out"]).reshape(B, N, D)
```
